# Optimizing a Trainium2 kernel written in Bass

```python
import numpy as np
import jax
import jax.numpy as jnp

def _softmax(x, axis=-1):
    return jax.nn.softmax(x, axis=axis)

def _gelu(x):
    return jax.nn.gelu(x, approximate=True)

def _silu(x):
    return jax.nn.silu(x)

def _sigmoid(x):
    return jax.nn.sigmoid(x)

def _layernorm(x, axis=-1, eps=1e-05):
    m = jnp.mean(x, axis=axis, keepdims=True)
    v = jnp.var(x, axis=axis, keepdims=True)
    return (x - m) / jnp.sqrt(v + eps)

def _scatter_add(tgt, idx, src, axis=0):
    return tgt.at[idx].add(src)

def _segment_sum(src, seg, n):
    return jax.ops.segment_sum(src, seg, n)
kernel_name = 'mk_vit_tower_postln_d1_tok_img768_r4_e4a4e9'

def setup_inputs(seed: int=0):
    np.random.seed(seed)
    _w = jnp.asarray

    def _rec_inputs():
        import jax
        import jax.numpy as jnp
        _rk = jax.random.key(seed)
        x = -0.000356955 + 1 * jax.random.normal(jax.random.fold_in(_rk, 1), (128, 3, 224, 224), jnp.float32)
        return x
    x = _rec_inputs()

    def _L0_tok_setup():
        import jax, jax.numpy as jnp
        import numpy as np
        N_PATCHES = 14
        HIDDEN_D = 192
        N_HEADS = 12
        D_HEAD = HIDDEN_D // N_HEADS
        SEQ = N_PATCHES ** 2 + 1
        INPUT_D = 3 * 16 * 16
        LN_EPS = 1e-05

        def positional_embeddings(seq_len, d):
            i = jnp.arange(seq_len, dtype=jnp.float32)[:, None]
            j = jnp.arange(d, dtype=jnp.float32)[None, :]
            even = (jnp.arange(d) % 2 == 0)[None, :]
            denom_even = jnp.power(10000.0, j / d)
            denom_odd = jnp.power(10000.0, (j - 1.0) / d)
            return jnp.where(even, jnp.sin(i / denom_even), jnp.cos(i / denom_odd))

        def _forward(images, W_map, b_map, class_token, ln_w, ln_b, Wq, bq, Wk, bk, Wv, bv):
            n = images.shape[0]
            patches = images.reshape(n, N_PATCHES ** 2, INPUT_D)
            tokens = jnp.einsum('npi,di->npd', patches, W_map) + b_map
            cls = jnp.broadcast_to(class_token[None], (n, 1, HIDDEN_D))
            tokens = jnp.concatenate([cls, tokens], axis=1)
            tokens = tokens + positional_embeddings(SEQ, HIDDEN_D)[None]
            mean = jnp.mean(tokens, axis=(-2, -1), keepdims=True)
            var = jnp.var(tokens, axis=(-2, -1), keepdims=True)
            x = (tokens - mean) / jnp.sqrt(var + LN_EPS) * ln_w + ln_b
            xh = x.reshape(n, SEQ, N_HEADS, D_HEAD)
            q = jnp.einsum('bshd,hed->bshe', xh, Wq) + bq[None, None]
            k = jnp.einsum('bshd,hed->bshe', xh, Wk) + bk[None, None]
            v = jnp.einsum('bshd,hed->bshe', xh, Wv) + bv[None, None]
            att = jax.nn.softmax(jnp.einsum('bshd,bthd->bhst', q, k) / jnp.sqrt(jnp.float32(D_HEAD)), axis=-1)
            msa = jnp.einsum('bhst,bthd->bshd', att, v).reshape(n, SEQ, HIDDEN_D)
            return tokens + msa
        key = jax.random.key(seed)
        ks = jax.random.split(key, 12)
        s = 0.02
        return {'images': jax.random.normal(ks[0], (128, 3, 224, 224), dtype=jnp.float32), 'W_map': jax.random.normal(ks[1], (HIDDEN_D, INPUT_D), dtype=jnp.float32) * s, 'b_map': jax.random.normal(ks[2], (HIDDEN_D,), dtype=jnp.float32) * s, 'class_token': jax.random.uniform(ks[3], (1, HIDDEN_D), dtype=jnp.float32), 'ln_w': jnp.ones((SEQ, HIDDEN_D), dtype=jnp.float32), 'ln_b': jnp.zeros((SEQ, HIDDEN_D), dtype=jnp.float32), 'Wq': jax.random.normal(ks[4], (N_HEADS, D_HEAD, D_HEAD), dtype=jnp.float32) * s, 'bq': jax.random.normal(ks[5], (N_HEADS, D_HEAD), dtype=jnp.float32) * s, 'Wk': jax.random.normal(ks[6], (N_HEADS, D_HEAD, D_HEAD), dtype=jnp.float32) * s, 'bk': jax.random.normal(ks[7], (N_HEADS, D_HEAD), dtype=jnp.float32) * s, 'Wv': jax.random.normal(ks[8], (N_HEADS, D_HEAD, D_HEAD), dtype=jnp.float32) * s, 'bv': jax.random.normal(ks[9], (N_HEADS, D_HEAD), dtype=jnp.float32) * s}
    _L0_tok_all = _L0_tok_setup()
    _L0_tok_in = {k: v for k, v in _L0_tok_all.items() if k in ('W_map', 'b_map', 'class_token', 'ln_w', 'ln_b', 'Wq', 'bq', 'Wk', 'bk', 'Wv', 'bv')}
    del _L0_tok_all

    def _L0_attn_setup():
        import jax, jax.numpy as jnp
        import numpy as np
        B, S, C = (2, 512, 192)
        H = 12
        D = C // H
        SCALE = D ** (-0.5)
        key = jax.random.key(seed)
        k1, k2, k3, k4 = jax.random.split(key, 4)
        std = C ** (-0.5)
        return {'x': jax.random.normal(k1, (B, S, C), jnp.float32), 'W_qkv': jax.random.normal(k2, (C, 3 * C), jnp.float32) * std, 'W_out': jax.random.normal(k3, (C, C), jnp.float32) * std, 'b_out': jax.random.normal(k4, (C,), jnp.float32) * 0.01}
    _L0_attn_all = _L0_attn_setup()
    _L0_attn_in = {k: v for k, v in _L0_attn_all.items() if k in ('W_qkv', 'W_out', 'b_out')}
    del _L0_attn_all

    def _L0_ffn_setup():
        import jax, jax.numpy as jnp
        import numpy as np
        EPS_NORM = 1e-05
        RMS_EPS = 1e-05

        def _l2_normalize(v):
            n = jnp.sqrt(jnp.sum(v * v, axis=-1, keepdims=True))
            return v / jnp.maximum(n, EPS_NORM)

        def _rms_norm(x, weight, eps):
            ms = jnp.mean(x * x, axis=-1, keepdims=True)
            return x * jax.lax.rsqrt(ms + eps) * weight
        key = jax.random.key(seed)
        ks = jax.random.split(key, 6)
        B, T, D = (8, 1024, 192)
        S, F = (64, 768)
        x = jax.random.normal(ks[0], (B, T, D), dtype=jnp.float32)
        slots = 0.02 * jax.random.normal(ks[1], (S, D), dtype=jnp.float32)
        scale = jnp.ones((S,), dtype=jnp.float32)
        fc1_weight = 0.02 * jax.random.normal(ks[2], (S, D, F), dtype=jnp.float32)
        fc1_bias = jnp.zeros((S, F), dtype=jnp.float32)
        fc2_weight = 0.02 * jax.random.normal(ks[3], (S, F, D), dtype=jnp.float32)
        fc2_bias = jnp.zeros((S, D), dtype=jnp.float32)
        norm_weight = jnp.ones((D,), dtype=jnp.float32)
        return {'x': x, 'slots': slots, 'scale': scale, 'fc1_weight': fc1_weight, 'fc1_bias': fc1_bias, 'fc2_weight': fc2_weight, 'fc2_bias': fc2_bias, 'norm_weight': norm_weight}
    _L0_ffn_all = _L0_ffn_setup()
    _L0_ffn_in = {k: v for k, v in _L0_ffn_all.items() if k in ('slots', 'scale', 'fc1_weight', 'fc1_bias', 'fc2_weight', 'fc2_bias', 'norm_weight')}
    del _L0_ffn_all
    return {'x': x, 'L0_tok_W_map': _L0_tok_in['W_map'], 'L0_tok_b_map': _L0_tok_in['b_map'], 'L0_tok_class_token': _L0_tok_in['class_token'], 'L0_tok_ln_w': _L0_tok_in['ln_w'], 'L0_tok_ln_b': _L0_tok_in['ln_b'], 'L0_tok_Wq': _L0_tok_in['Wq'], 'L0_tok_bq': _L0_tok_in['bq'], 'L0_tok_Wk': _L0_tok_in['Wk'], 'L0_tok_bk': _L0_tok_in['bk'], 'L0_tok_Wv': _L0_tok_in['Wv'], 'L0_tok_bv': _L0_tok_in['bv'], 'L0_attn_W_qkv': _L0_attn_in['W_qkv'], 'L0_attn_W_out': _L0_attn_in['W_out'], 'L0_attn_b_out': _L0_attn_in['b_out'], 'L0_ffn_slots': _L0_ffn_in['slots'], 'L0_ffn_scale': _L0_ffn_in['scale'], 'L0_ffn_fc1_weight': _L0_ffn_in['fc1_weight'], 'L0_ffn_fc1_bias': _L0_ffn_in['fc1_bias'], 'L0_ffn_fc2_weight': _L0_ffn_in['fc2_weight'], 'L0_ffn_fc2_bias': _L0_ffn_in['fc2_bias'], 'L0_ffn_norm_weight': _L0_ffn_in['norm_weight']}

def reference(x, L0_tok_W_map, L0_tok_b_map, L0_tok_class_token, L0_tok_ln_w, L0_tok_ln_b, L0_tok_Wq, L0_tok_bq, L0_tok_Wk, L0_tok_bk, L0_tok_Wv, L0_tok_bv, L0_attn_W_qkv, L0_attn_W_out, L0_attn_b_out, L0_ffn_slots, L0_ffn_scale, L0_ffn_fc1_weight, L0_ffn_fc1_bias, L0_ffn_fc2_weight, L0_ffn_fc2_bias, L0_ffn_norm_weight):
    import jax
    import jax.numpy as jnp

    def _L0_tok_ref(images, W_map, b_map, class_token, ln_w, ln_b, Wq, bq, Wk, bk, Wv, bv):
        import jax, jax.numpy as jnp
        import numpy as np
        N_PATCHES = 14
        HIDDEN_D = 192
        N_HEADS = 12
        D_HEAD = HIDDEN_D // N_HEADS
        SEQ = N_PATCHES ** 2 + 1
        INPUT_D = 3 * 16 * 16
        LN_EPS = 1e-05

        def positional_embeddings(seq_len, d):
            i = jnp.arange(seq_len, dtype=jnp.float32)[:, None]
            j = jnp.arange(d, dtype=jnp.float32)[None, :]
            even = (jnp.arange(d) % 2 == 0)[None, :]
            denom_even = jnp.power(10000.0, j / d)
            denom_odd = jnp.power(10000.0, (j - 1.0) / d)
            return jnp.where(even, jnp.sin(i / denom_even), jnp.cos(i / denom_odd))

        def _forward(images, W_map, b_map, class_token, ln_w, ln_b, Wq, bq, Wk, bk, Wv, bv):
            n = images.shape[0]
            patches = images.reshape(n, N_PATCHES ** 2, INPUT_D)
            tokens = jnp.einsum('npi,di->npd', patches, W_map) + b_map
            cls = jnp.broadcast_to(class_token[None], (n, 1, HIDDEN_D))
            tokens = jnp.concatenate([cls, tokens], axis=1)
            tokens = tokens + positional_embeddings(SEQ, HIDDEN_D)[None]
            mean = jnp.mean(tokens, axis=(-2, -1), keepdims=True)
            var = jnp.var(tokens, axis=(-2, -1), keepdims=True)
            x = (tokens - mean) / jnp.sqrt(var + LN_EPS) * ln_w + ln_b
            xh = x.reshape(n, SEQ, N_HEADS, D_HEAD)
            q = jnp.einsum('bshd,hed->bshe', xh, Wq) + bq[None, None]
            k = jnp.einsum('bshd,hed->bshe', xh, Wk) + bk[None, None]
            v = jnp.einsum('bshd,hed->bshe', xh, Wv) + bv[None, None]
            att = jax.nn.softmax(jnp.einsum('bshd,bthd->bhst', q, k) / jnp.sqrt(jnp.float32(D_HEAD)), axis=-1)
            msa = jnp.einsum('bhst,bthd->bshd', att, v).reshape(n, SEQ, HIDDEN_D)
            return tokens + msa
        return _forward(images, W_map, b_map, class_token, ln_w, ln_b, Wq, bq, Wk, bk, Wv, bv)

    def _L0_attn_ref(x, W_qkv, W_out, b_out):
        import jax, jax.numpy as jnp
        import numpy as np
        B, S, C = (2, 512, 192)
        H = 12
        D = C // H
        SCALE = D ** (-0.5)
        Bx, Sx, _ = x.shape
        qkv = (x @ W_qkv).reshape(Bx, Sx, 3, H, D).transpose(2, 0, 3, 1, 4)
        q, k, v = (qkv[0], qkv[1], qkv[2])
        att = jnp.einsum('bhxd,bhyd->bhxy', q, k) * SCALE
        causal_mask = jnp.tril(jnp.ones((Sx, Sx), bool))
        att = jnp.where(causal_mask[None, None], att, -jnp.inf)
        att = jax.nn.softmax(att, axis=-1)
        out = jnp.einsum('bhxy,bhyd->bhxd', att, v)
        out = out.transpose(0, 2, 1, 3).reshape(Bx, Sx, H * D)
        return out @ W_out + b_out

    def _L0_ffn_ref(x, slots, scale, fc1_weight, fc1_bias, fc2_weight, fc2_bias, norm_weight):
        import jax, jax.numpy as jnp
        import numpy as np
        EPS_NORM = 1e-05
        RMS_EPS = 1e-05

        def _l2_normalize(v):
            n = jnp.sqrt(jnp.sum(v * v, axis=-1, keepdims=True))
            return v / jnp.maximum(n, EPS_NORM)

        def _rms_norm(x, weight, eps):
            ms = jnp.mean(x * x, axis=-1, keepdims=True)
            return x * jax.lax.rsqrt(ms + eps) * weight
        xn = _rms_norm(x, norm_weight, RMS_EPS)
        tok = _l2_normalize(xn)
        sl = _l2_normalize(slots) * scale[:, None]
        logits = jnp.einsum('sd,btd->bst', sl, tok)
        dispatch_w = jax.nn.softmax(logits, axis=-1)
        combine_w = jax.nn.softmax(logits, axis=-2)
        y = jnp.einsum('btd,bst->bsd', xn, dispatch_w)
        y = jnp.einsum('sio,bsi->bso', fc1_weight, y) + fc1_bias
        y = jax.nn.gelu(y, approximate=False)
        y = jnp.einsum('sio,bsi->bso', fc2_weight, y) + fc2_bias
        out = jnp.einsum('bsd,bst->btd', y, combine_w)
        return out
    h = _L0_tok_ref(x, L0_tok_W_map, L0_tok_b_map, L0_tok_class_token, L0_tok_ln_w, L0_tok_ln_b, L0_tok_Wq, L0_tok_bq, L0_tok_Wk, L0_tok_bk, L0_tok_Wv, L0_tok_bv)
    h = _layernorm(h + _L0_attn_ref(h, L0_attn_W_qkv, L0_attn_W_out, L0_attn_b_out), axis=-1)
    h = _layernorm(h + _L0_ffn_ref(h, L0_ffn_slots, L0_ffn_scale, L0_ffn_fc1_weight, L0_ffn_fc1_bias, L0_ffn_fc2_weight, L0_ffn_fc2_bias, L0_ffn_norm_weight), axis=-1)
    return h

_drawn_inputs = setup_inputs


def setup_inputs(seed=0):
    import zlib

    import numpy as np

    out = dict(_drawn_inputs(seed))
    spreads = {'L0_tok_ln_w': (1.0, 0.6),
     'L0_tok_ln_b': (0.0, 2.0),
     'L0_ffn_scale': (1.0, 0.6),
     'L0_ffn_fc1_bias': (0.0, 0.8),
     'L0_ffn_fc2_bias': (0.0, 0.694),
     'L0_ffn_norm_weight': (1.0, 0.6)}
    factors = {'L0_tok_Wq': 8.0,
     'L0_tok_bq': 32.806,
     'L0_tok_Wk': 8.0,
     'L0_tok_bk': 64.0,
     'L0_attn_b_out': 5.998,
     'L0_ffn_slots': 8.0,
     'L0_ffn_fc1_weight': 8.0,
     'L0_ffn_fc2_weight': 7.554,
     'L0_tok_class_token': 3.074}
    for name, (base, spread) in spreads.items():
        noise = np.random.default_rng([zlib.crc32(name.encode()), seed]).standard_normal(out[name].shape)
        drawn = base * np.exp(spread * noise) if base else spread * noise
        out[name] = jnp.asarray(drawn.astype(out[name].dtype))
    for name, factor in factors.items():
        out[name] = (out[name] * factor).astype(out[name].dtype)
    return out
```

```python
from contextlib import ExitStack

import concourse.bass as bass
import numpy as np
from concourse import mybir

F32 = mybir.dt.float32
BF16 = mybir.dt.bfloat16
ALU = mybir.AluOpType
ACT = mybir.ActivationFunctionType
AX = mybir.AxisListType

D = 192
HEADS = 12
DH = D // HEADS
CH = D // 2
HC = HEADS // 2
SEQ = 197
TT = 99
SP = 2 * TT
PATCHES = SEQ - 1
PT = PATCHES // 2
INPUT = 768
KC = INPUT // 128
SLOTS = 64
FF = 768
FC = FF // 128
PARTS = 3
Q_SLOTS = (0, 0, 1, 0, 2, 1)
K_SLOTS = (0, 1, 0, 2, 0, 1)
STACK = len(Q_SLOTS) * DH
AUG = STACK + PARTS
SCALES = (0.25, 1.0)
LN_EPS = 1e-5
READY1 = 8
MASKED = -3e38
G = 4
NG = HEADS // G


class Image:

    def __init__(self, turn, place, R):
        self.turn, self.place, self.R = turn, place, R

    def __sub__(self, s):
        at = self.place - s
        return Image(self.turn + at // self.R, at % self.R, self.R)

    @property
    def number(self):
        return self.turn * self.R + self.place

    @property
    def parity(self):
        return self.place % 2

    def inside(self, n):
        return not isinstance(self.turn, int) or 0 <= self.number < n


class Event:

    def __init__(self, sem, n, R):
        self.sem, self.n, self.R = sem, n, R

    def seed(self, eng):
        eng.sem_inc(self.sem, self.R * self.n)

    def at(self, image, k=None):
        return image.number * self.n + (self.R * self.n + (self.n if k is None else k))


class Transfers:

    def __init__(self, sems, n):
        self.sems, self.n = sems, 16 * n

    def seed(self, eng):
        for sem in self.sems:
            eng.sem_inc(sem, self.n)

    def of(self, image):
        return self.sems[image.place]

    def at(self, image):
        return (image.turn + 2) * self.n


def pipeline(eng, n, depth, R, step):
    head = depth + (n - depth) % R
    for c in range(head):
        step(Image(c // R, c % R, R))
    if n > head:
        with eng.Fori(0, (n - head) // R) as j:
            for c in range(head, head + R):
                step(Image(j + c // R, c % R, R))
    for c in range(n, n + depth):
        step(Image(c // R, c % R, R))


class Memory:

    def __init__(self, nc, ctx, R):
        self.nc, self.ctx, self.R, self.sems = nc, ctx, R, []
        self.held = self.sem(f"held{nc.next_id()}")
        ctx.callback(self.release)

    def sb(self, name, shape, dt=F32):
        return self.ctx.enter_context(self.nc.sbuf_tensor(name, shape, dt))

    def ps(self, name, shape, dt=F32):
        return self.ctx.enter_context(self.nc.psum_tensor(name, shape, dt))

    def sem(self, name):
        self.sems.append(self.nc.alloc_semaphore(name=name))
        return self.sems[-1]

    def hold(self, eng):
        eng.sem_inc(self.held, 1)

    def release(self):
        self.nc.clear_and_free_semaphores(self.sems)
        self.nc.all_engine_barrier()

    def event(self, name, n=1):
        return Event(self.sem(name), n, self.R)

    def transfers(self, name, n=1):
        return Transfers([self.sem(f"{name}{i}") for i in range(self.R)], n)


def split_high(act, parts, psum, scale):
    return act.activation(parts, psum, ACT.Copy, scale=scale)


def embed_pass(nc, n, A, scr):
    R = 4
    with ExitStack() as ctx:
        m = Memory(nc, ctx, R)
        patches = m.sb("e_patches", [PT, R, 2, INPUT])
        wmap = m.sb("e_wmap", [128, KC, D])
        wqkv = m.sb("e_wqkv", [CH + 1, 3, 2, CH])
        posb = m.sb("e_posb", [TT, 2, D])
        rowb = m.sb("e_rowb", [TT, 2, D])
        lnw = m.sb("e_lnw", [TT, 2, D])
        lnb = m.sb("e_lnb", [TT, 2, D])
        ident = m.sb("e_ident", [128, 128])
        cmean = m.sb("e_cmean", [TT, TT])
        cvar = m.sb("e_cvar", [TT, 2, TT])
        eps = m.sb("e_eps", [TT, 1])
        ptT = m.sb("e_ptT", [128, 2, KC, SP])
        tv = m.sb("e_tv", [TT, R, 2, 2, D])
        xc = m.sb("e_xc", [TT, 2, 2, D])
        xn = m.sb("e_xn", [TT, 2, 2, D])
        junk = m.sb("e_junk", [TT, 2, D])
        xT = m.sb("e_xT", [CH + 1, 2, 2, SP])
        rest = m.sb("e_rest", [CH, 2, 2, 2, SP])
        parts = m.sb("e_parts", [CH, R, 2, PARTS, 2, SP], BF16)
        st = m.sb("e_st", [TT, 2, 8])
        tpp = [m.ps(f"e_tp{i}", [128, 2, PATCHES]) for i in range(3)]
        tokp = m.ps("e_tokp", [TT, 2, D])
        statp = m.ps("e_statp", [TT, 2])
        xtp = m.ps("e_xtp", [128, 512])
        qp = m.ps("e_qp", [CH, 2, SP])
        kp = m.ps("e_kp", [CH, 2, SP])
        vp = xtp[0:TT, 0:2 * D].rearrange("p (t d) -> p t d", t=2)
        xtv = xtp[0:CH, 0:2 * SP].rearrange("p (c s) -> p c s", c=2)

        const = m.sem("e_const")
        ready = m.sem("e_ready")
        loaded = m.transfers("e_loaded")
        turned = m.event("e_turned", 3)
        turned_a = m.event("e_turned_a", 2)
        turned_v = m.event("e_turned_v", 1)
        embedded = m.event("e_embedded")
        tokens = m.event("e_tokens")
        mean_p = m.event("e_mean_p")
        mean_s = m.event("e_mean_s")
        squares = m.event("e_squares", 2)
        var_p = m.event("e_var_p")
        std = m.event("e_std")
        rstd = m.event("e_rstd")
        centred = m.event("e_centred")
        normed = m.event("e_normed")
        x_turned = m.event("e_x_turned")
        x_copied = m.event("e_x_copied")
        q_done = m.event("e_q_done")
        k_done = m.event("e_k_done")
        v_done = m.event("e_v_done")
        v_copied = m.event("e_v_copied")
        high = m.event("e_high", 2)
        left = m.event("e_left", 2)
        middle = m.event("e_middle", 2)
        low = m.event("e_low", 2)
        stored = m.transfers("e_stored", 3)

        block = ctx.enter_context(nc.Block())

        @block.sync
        def _(sp):
            loads = [(wmap[:], A["wmapT"].rearrange("(k p) d -> p k d", p=128)), (wqkv[:], A["wqkv1"]),
                     (posb[:], A["pos"].rearrange("(t p) d -> p t d", p=TT)),
                     (rowb[:], A["rowb"].rearrange("(t p) d -> p t d", p=TT)),
                     (lnw[:], A["lnw"].rearrange("(t p) d -> p t d", p=TT)),
                     (lnb[:], A["lnb"].rearrange("(t p) d -> p t d", p=TT)), (ident[:], A["ident"])]
            for e in (loaded, stored):
                e.seed(sp)
            for to, of in loads:
                sp.dma_start(to, of).then_inc(const, 16)

            def step(c):
                if c.inside(n):
                    sp.wait_ge(turned.sem, turned.at(c - 4))
                    sp.dma_start(patches[:, c.place], A["x"][c.number].rearrange("(t p) i -> p t i", t=2)).then_inc(loaded.of(c), 16)
                b = c - 3
                if b.inside(n):
                    sp.wait_ge(v_copied.sem, v_copied.at(b))
                    sp.dma_start(scr["tv1"][b.number], tv[:, b.place]).then_inc(stored.of(b), 16)
                    for i in range(2):
                        sp.wait_ge(low.sem, low.at(b, i + 1))
                        sp.dma_start(scr["qk1"][b.number, i].rearrange("a (c p) s -> p (a c) s", p=CH),
                                     parts[:, b.place, i].rearrange("p a c s -> p (a c) s")).then_inc(stored.of(b), 16)
            pipeline(sp, n, 3, R, step)
            for i in range(n - R, n):
                sp.wait_ge(stored.of(Image(i // R, i % R, R)), stored.at(Image(i // R, i % R, R)))

        @block.gpsimd
        def _(pool):
            for e in (middle, low):
                e.seed(pool)

            def step(c):
                c = c - 1
                u = c.parity
                b = c - 2
                if b.inside(n):
                    for i in range(2):
                        pool.wait_ge(left.sem, left.at(b, i + 1))
                        pool.wait_ge(stored.of(b - 4), stored.at(b - 4))
                        m.hold(pool)
                        pool.tensor_copy(parts[:, b.place, i, 1], rest[:, u, i]).then_inc(middle.sem, 1)
                        pool.wait_ge(middle.sem, middle.at(b, i + 1))
                        pool.tensor_tensor(parts[:, b.place, i, 2], rest[:, u, i], parts[:, b.place, i, 1],
                                           ALU.subtract).then_inc(low.sem, 1)
            pipeline(pool, n, 3, R, step)

        @block.scalar
        def _(act):
            for e in (turned_a, squares, std, x_copied, high):
                e.seed(act)
            act.wait_ge(const, 16 * 7)
            act.wait_ge(ready, READY1)

            def step(c):
                c = c - 1
                u = c.parity
                b = c - 2
                if b.inside(n):
                    act.wait_ge(x_turned.sem, x_turned.at(b))
                    nc.scalar.copy(xT[0:CH, u], xtv).then_inc(x_copied.sem, 1)
                if c.inside(n):
                    for i in range(2):
                        act.wait_ge(turned.sem, turned.at(c, i + 1))
                        nc.scalar.copy(ptT[:, u, 2 * i:2 * i + 2, 1:1 + PATCHES], tpp[i][:]).then_inc(turned_a.sem, 1)
                b = c - 1
                w = 1 - u
                if b.inside(n):
                    act.wait_ge(mean_s.sem, mean_s.at(b))
                    for t in range(2):
                        nc.scalar.activation(junk[:, t], tv[:, b.place, 0, t], ACT.Square, bias=st[:, w, 1:2],
                                             accum_out=st[:, w, 2 + t:3 + t]).then_inc(squares.sem, 1)
                b = c - 2
                if b.inside(n):
                    act.wait_ge(stored.of(b - 4), stored.at(b - 4))
                    for i, (done, p) in enumerate(((q_done, qp), (k_done, kp))):
                        act.wait_ge(done.sem, done.at(b))
                        split_high(nc.scalar, parts[:, b.place, i, 0], p[:], SCALES[i]).then_inc(high.sem, 1)
                b = c - 1
                if b.inside(n):
                    act.wait_ge(var_p.sem, var_p.at(b))
                    nc.scalar.activation(st[:, w, 4:5], statp[:, 1:2], ACT.Sqrt, bias=eps[:, 0:1]).then_inc(std.sem, 1)
            pipeline(act, n, 3, R, step)

        @block.vector
        def _(dve):
            for e in (turned_v, tokens, mean_s, rstd, centred, normed, v_copied, left):
                e.seed(dve)
            dve.wait_ge(const, 16 * 7)
            nc.vector.memset(ptT[:], 0.0).then_inc(ready, 1)
            nc.vector.memset(xT[CH:CH + 1], 1.0).then_inc(ready, 1)
            nc.vector.memset(cmean[:], -1.0 / (SEQ * D)).then_inc(ready, 1)
            nc.vector.memset(cvar[:], 0.0).then_inc(ready, 1)
            nc.vector.memset(eps[:], LN_EPS).then_inc(ready, 1)
            nc.vector.tensor_tensor(posb[:], posb[:], rowb[:], ALU.add).then_inc(ready, 1)
            dve.wait_ge(ready, READY1 - 2)
            nc.vector.tensor_scalar(cvar[0:TT, 0], cvar[0:TT, 0], 1.0 / (SEQ * D), None, ALU.add).then_inc(ready, 1)
            nc.vector.tensor_scalar(cvar[0:TT - 1, 1], cvar[0:TT - 1, 1], 1.0 / (SEQ * D), None, ALU.add).then_inc(ready, 1)
            dve.wait_ge(ready, READY1)

            def step(c):
                c = c - 1
                u = c.parity
                w = 1 - u
                b = c - 1
                if b.inside(n):
                    dve.wait_ge(embedded.sem, embedded.at(b))
                    dve.wait_ge(stored.of(b - 4), stored.at(b - 4))
                    nc.vector.scalar_tensor_tensor(out=tv[:, b.place, 0], in0=tokp[:], scalar=1.0, in1=posb[:],
                                                   op0=ALU.mult, op1=ALU.add,
                                                   accum_out=st[:, w, 0:1]).then_inc(tokens.sem, 1)
                if c.inside(n):
                    dve.wait_ge(turned.sem, turned.at(c, 3))
                    nc.vector.tensor_copy(ptT[:, u, 4:6, 1:1 + PATCHES], tpp[2][:]).then_inc(turned_v.sem, 1)
                if b.inside(n):
                    dve.wait_ge(mean_p.sem, mean_p.at(b))
                    nc.vector.tensor_copy(st[:, w, 1:2], statp[:, 0:1]).then_inc(mean_s.sem, 1)
                    dve.wait_ge(mean_s.sem, mean_s.at(b))
                    nc.vector.scalar_tensor_tensor(out=xc[:, w], in0=tv[:, b.place, 0], scalar=st[:, w, 1:2], in1=lnw[:],
                                                   op0=ALU.add, op1=ALU.mult).then_inc(centred.sem, 1)
                b2 = c - 2
                if b2.inside(n):
                    for i, (done, p) in enumerate(((q_done, qp), (k_done, kp))):
                        dve.wait_ge(high.sem, high.at(b2, i + 1))
                        dve.wait_ge(low.sem, low.at(b2 - 2, i + 1))
                        nc.vector.scalar_tensor_tensor(out=rest[:, u, i], in0=p[:], scalar=SCALES[i],
                                                       in1=parts[:, b2.place, i, 0], op0=ALU.mult,
                                                       op1=ALU.subtract).then_inc(left.sem, 1)
                    dve.wait_ge(v_done.sem, v_done.at(b2))
                    nc.vector.tensor_copy(tv[:, b2.place, 1], vp).then_inc(v_copied.sem, 1)
                if b.inside(n):
                    dve.wait_ge(std.sem, std.at(b))
                    nc.vector.reciprocal(st[:, w, 5:6], st[:, w, 4:5]).then_inc(rstd.sem, 1)
                    dve.wait_ge(rstd.sem, rstd.at(b))
                    dve.wait_ge(centred.sem, centred.at(b))
                    nc.vector.scalar_tensor_tensor(out=xn[:, w], in0=xc[:, w], scalar=st[:, w, 5:6], in1=lnb[:],
                                                   op0=ALU.mult, op1=ALU.add).then_inc(normed.sem, 1)
            pipeline(dve, n, 3, R, step)

        @block.tensor
        def _(pe):
            for e in (turned, embedded, mean_p, var_p, x_turned, q_done, k_done, v_done):
                e.seed(pe)
            pe.wait_ge(const, 16 * 7)
            pe.wait_ge(ready, READY1)

            def step(c):
                c = c - 1
                u = c.parity
                w = 1 - u
                b1, b2 = c - 1, c - 2
                if b1.inside(n):
                    pe.wait_ge(turned_a.sem, turned_a.at(b1))
                    pe.wait_ge(turned_v.sem, turned_v.at(b1))
                    pe.wait_ge(tokens.sem, tokens.at(b1 - 1))
                    for t in range(2):
                        for k in range(KC):
                            mm = nc.tensor.matmul(tokp[:, t], ptT[:, w, k, t * TT:(t + 1) * TT], wmap[:, k],
                                                  start=(k == 0), stop=(k == KC - 1))
                    mm.then_inc(embedded.sem, 1)
                if b2.inside(n):
                    pe.wait_ge(normed.sem, normed.at(b2))
                    pe.wait_ge(v_copied.sem, v_copied.at(b2 - 1))
                    for t in range(2):
                        for h in range(2):
                            mm = nc.tensor.transpose(xtv[:, h, t * TT:(t + 1) * TT],
                                                     xn[:, u, t, h * CH:(h + 1) * CH], ident[0:TT, 0:TT])
                    mm.then_inc(x_turned.sem, 1)
                if c.inside(n):
                    pe.wait_ge(loaded.of(c), loaded.at(c))
                    for i in range(3):
                        if i < 2:
                            pe.wait_ge(turned_a.sem, turned_a.at(c - 1, i + 1))
                        else:
                            pe.wait_ge(turned_v.sem, turned_v.at(c - 1))
                        for k in range(2):
                            for t in range(2):
                                mm = nc.tensor.transpose(tpp[i][:, k, t * PT:(t + 1) * PT],
                                                         patches[:, c.place, t, (2 * i + k) * 128:(2 * i + k + 1) * 128],
                                                         ident[0:PT, 0:PT])
                        mm.then_inc(turned.sem, 1)
                if b1.inside(n):
                    pe.wait_ge(tokens.sem, tokens.at(b1))
                    pe.wait_ge(std.sem, std.at(b1 - 1))
                    nc.tensor.matmul(statp[:, 0:1], cmean[:], st[:, w, 0:1], start=True, stop=True).then_inc(mean_p.sem, 1)
                if b2.inside(n):
                    pe.wait_ge(x_copied.sem, x_copied.at(b2))
                    for i, (done, p) in enumerate(((q_done, qp), (k_done, kp))):
                        pe.wait_ge(left.sem, left.at(b2 - 1, i + 1))
                        for h in range(2):
                            mm = nc.tensor.matmul(p[:, h], wqkv[:, i, h], xT[:, u, h], start=True, stop=True)
                        mm.then_inc(done.sem, 1)
                    for t in range(2):
                        for h in range(2):
                            mm = nc.tensor.matmul(vp[:, t, h * CH:(h + 1) * CH], xT[:, u, h, t * TT:(t + 1) * TT],
                                                  wqkv[:, 2, h], start=True, stop=True)
                    mm.then_inc(v_done.sem, 1)
                if b1.inside(n):
                    pe.wait_ge(squares.sem, squares.at(b1))
                    for t in range(2):
                        mm = nc.tensor.matmul(statp[:, 1:2], cvar[:, t], st[:, w, 2 + t:3 + t],
                                              start=(t == 0), stop=(t == 1))
                    mm.then_inc(var_p.sem, 1)
            pipeline(pe, n, 3, R, step)


def attend_pass(nc, n, A, scr, causal):
    R = 4
    X = "c_" if causal else "a_"
    qk_in, tv_in = (scr["qk2"], scr["tv2"]) if causal else (scr["qk1"], scr["tv1"])
    with ExitStack() as ctx:
        m = Memory(nc, ctx, R)
        qs = m.sb(X + "qs", [AUG, R, HEADS, SP], BF16)
        ks = m.sb(X + "ks", [AUG, R, HEADS, SP], BF16)
        tv = m.sb(X + "tv", [TT, R, 2, 2, D])
        vx = m.sb(X + "vx", [TT, R, 2, HEADS, 32])
        mx = m.sb(X + "mx", [TT, 2, 2, HEADS])
        mxp = m.sb(X + "mxp", [HEADS, 2, PARTS, SP], BF16)
        mxr = m.sb(X + "mxr", [HEADS, 2, SP])
        ex = m.sb(X + "ex", [TT, NG, 2, G * SP])
        ot = m.sb(X + "ot", [128, 2, NG, SP])
        rec = m.sb(X + "rec", [TT, 2, HEADS])
        on = m.sb(X + "on", [TT, 2, 2, D])
        hT = m.sb(X + "hT", [CH, 2, SP])
        ident = m.sb(X + "ident", [128, 128])
        res = m.sb(X + "res", [TT, 2, 2, 2, D])
        if causal:
            wout = m.sb(X + "wout", [CH, 2, D])
            bout = m.sb(X + "bout", [TT, 1, D])
            bout2 = m.sb(X + "bout2", [TT, 2, D])
            masks = m.sb(X + "masks", [TT, 2, TT])
            maskb = m.sb(X + "maskb", [TT, 2, TT], BF16)
            identb = m.sb(X + "identb", [TT, TT], BF16)
        else:
            wqkv = m.sb(X + "wqkv", [CH, 2, 3 * D])
            rest = m.sb(X + "rest", [CH, 2, 2, SP])
            parts = m.sb(X + "parts", [CH, 2, 2, PARTS, 2, SP], BF16)

        sq = [m.ps(f"{X}sq{i}", [TT, 2, SP]) for i in range(2)]
        sk = [m.ps(f"{X}sk{i}", [TT, 2, 512]) for i in range(2)]
        pvp = m.ps(X + "pvp", [128, 512])
        work = m.ps(X + "work", [128, 512])
        pv = pvp[:, 0:SP]
        vp = pvp[0:TT, 0:2 * D].rearrange("p (t d) -> p t d", t=2)
        mxT = work[0:HEADS, 0:SP]
        oT = work[0:TT, 0:NG * 128]
        onT = work[0:CH, 0:2 * SP].rearrange("p (c s) -> p c s", c=2)
        proj = work[0:TT, 0:2 * D].rearrange("p (t d) -> p t d", t=2)

        const = m.sem(X + "const")
        ready = m.sem(X + "ready")
        qk_in_place = m.transfers(X + "qk_in_place", 12)
        tv_in_place = m.transfers(X + "tv_in_place")
        scored_q = m.event(X + "scored_q", 12)
        maxed = m.event(X + "maxed", 12)
        max_turned = m.event(X + "max_turned")
        max_high = m.event(X + "max_high")
        max_rest = m.event(X + "max_rest")
        max_mid = m.event(X + "max_mid")
        max_low = m.event(X + "max_low")
        max_in_place = m.transfers(X + "max_in_place", 3)
        v_spread = m.event(X + "v_spread")
        scored_k = m.event(X + "scored_k", 6)
        exped = m.event(X + "exped", 6)
        summed = m.event(X + "summed", 3)
        o_copied = m.event(X + "o_copied", 3)
        o_turned = m.event(X + "o_turned", 2)
        recip = m.event(X + "recip", 2)
        o_normed = m.event(X + "o_normed", 2)
        added = m.event(X + "added")
        h_turned = m.event(X + "h_turned")
        h_copied = m.event(X + "h_copied")
        done = m.event(X + "done", 1 if causal else 3)
        high = m.event(X + "high", 2)
        left = m.event(X + "left", 2)
        middle = m.event(X + "middle", 2)
        low = m.event(X + "low", 2)
        finished = m.event(X + "finished")
        stored = m.transfers(X + "stored", 1 if causal else 3)
        block = ctx.enter_context(nc.Block())

        n_const, n_ready = (5 * 16, 7) if causal else (2 * 16, 3)

        def heads_of(fill):
            return fill // 6, 2 * (fill % 6)

        @block.sync
        def _(sp):
            for e in (qk_in_place, tv_in_place, max_in_place, stored):
                e.seed(sp)
            loads = [(ident[:], A["ident"])]
            if causal:
                loads += [(wout[:], A["wout"].rearrange("(c p) d -> p c d", p=CH)), (bout[:, 0], A["bout"]),
                          (masks[:, 0], A["above"]), (masks[:, 1], A["aboveT"])]
            else:
                loads += [(wqkv[:], A["wqkv2"].rearrange("(c p) d -> p c d", p=CH))]
            for to, of in loads:
                sp.dma_start(to, of).then_inc(const, 16)

            def step(c):
                b = c - 3
                if b.inside(n):
                    sp.wait_ge(max_low.sem, max_low.at(b))
                    for a in range(PARTS):
                        sp.dma_start(qs[STACK + a:STACK + a + 1, b.place], mxp[:, b.parity, a]).then_inc(max_in_place.of(b), 16)
                b = c - 5
                if b.inside(n):
                    sp.wait_ge(finished.sem, finished.at(b))
                    if causal:
                        sp.dma_start(scr["h_pre"][b.number], res[:, b.parity, 0]).then_inc(stored.of(b), 16)
                    else:
                        sp.wait_ge(added.sem, added.at(b))
                        sp.dma_start(scr["tv2"][b.number], res[:, b.parity]).then_inc(stored.of(b), 16)
                        for i in range(2):
                            sp.wait_ge(low.sem, low.at(b, i + 1))
                            sp.dma_start(scr["qk2"][b.number, i].rearrange("a (c p) s -> p (a c) s", p=CH),
                                         parts[:, b.parity, i].rearrange("p a c s -> p (a c) s")).then_inc(stored.of(b), 16)
                if c.inside(n):
                    sp.wait_ge(scored_k.sem, scored_k.at(c - 4))
                    for i, (stack, slots) in enumerate(((qs, Q_SLOTS), (ks, K_SLOTS))):
                        for s, a in enumerate(slots):
                            sp.dma_start(stack[s * DH:(s + 1) * DH, c.place],
                                         qk_in[c.number, i, a].rearrange("(h d) s -> d h s", d=DH)).then_inc(qk_in_place.of(c), 16)
                b = c - 1
                if b.inside(n):
                    sp.wait_ge(added.sem, added.at(b - 4))
                    sp.wait_ge(v_spread.sem, v_spread.at(b - 4))
                    sp.dma_start(tv[:, b.place], tv_in[b.number]).then_inc(tv_in_place.of(b), 16)
            pipeline(sp, n, 5, R, step)
            for i in range(n - R, n):
                sp.wait_ge(stored.of(Image(i // R, i % R, R)), stored.at(Image(i // R, i % R, R)))

        @block.gpsimd
        def _(pool):
            for e in (max_mid, max_low, v_spread, added, middle, low):
                e.seed(pool)
            pool.wait_ge(ready, n_ready)

            def step(c):
                b = c - 3
                if b.inside(n):
                    pool.wait_ge(max_rest.sem, max_rest.at(b))
                    pool.wait_ge(max_in_place.of(b - 2), max_in_place.at(b - 2))
                    pool.wait_ge((added if causal else low).sem, (added if causal else low).at(c - 6))
                    m.hold(pool)
                    pool.tensor_copy(mxp[:, b.parity, 1], mxr[:, b.parity]).then_inc(max_mid.sem, 1)
                    pool.wait_ge(max_mid.sem, max_mid.at(b))
                    pool.tensor_tensor(mxp[:, b.parity, 2], mxr[:, b.parity], mxp[:, b.parity, 1],
                                       ALU.subtract).then_inc(max_low.sem, 1)
                    pool.wait_ge(tv_in_place.of(b), tv_in_place.at(b))
                    pool.wait_ge(summed.sem, summed.at(b - 4))
                    pool.wait_ge(max_low.sem, max_low.at(b))
                    m.hold(pool)
                    pool.tensor_copy(vx[:, b.place, :, :, 0:DH],
                                     tv[:, b.place, 1].rearrange("p t (h d) -> p t h d", d=DH)).then_inc(v_spread.sem, 1)
                b = c - 5
                if b.inside(n):
                    if (c - 3).inside(n):
                        pool.wait_ge(v_spread.sem, v_spread.at(c - 3))
                    pool.wait_ge(stored.of(b - 2), stored.at(b - 2))
                    if causal:
                        pool.wait_ge(tv_in_place.of(b), tv_in_place.at(b))
                        pool.tensor_tensor(res[:, b.parity, 1], tv[:, b.place, 0], bout2[:],
                                           ALU.add).then_inc(added.sem, 1)
                    else:
                        pool.wait_ge(o_normed.sem, o_normed.at(b))
                        pool.tensor_tensor(res[:, b.parity, 0], tv[:, b.place, 0], on[:, b.parity],
                                           ALU.add).then_inc(added.sem, 1)
                        for i in range(2):
                            pool.wait_ge(left.sem, left.at(b, i + 1))
                            if i:
                                pool.wait_ge(low.sem, low.at(b, i))
                            else:
                                pool.wait_ge(added.sem, added.at(b))
                            m.hold(pool)
                            pool.tensor_copy(parts[:, b.parity, i, 1], rest[:, i]).then_inc(middle.sem, 1)
                            pool.wait_ge(middle.sem, middle.at(b, i + 1))
                            pool.tensor_tensor(parts[:, b.parity, i, 2], rest[:, i], parts[:, b.parity, i, 1],
                                               ALU.subtract).then_inc(low.sem, 1)
            pipeline(pool, n, 5, R, step)

        @block.scalar
        def _(act):
            for e in (exped, h_copied, high):
                e.seed(act)
            if not causal:
                finished.seed(act)

            def step(c):
                b4, b5 = c - 4, c - 5
                for k in range(6):
                    if b4.inside(n):
                        g, kt = k // 2, k % 2
                        rows = TT - kt
                        act.wait_ge(scored_k.sem, scored_k.at(b4, k + 1))
                        act.wait_ge(summed.sem, summed.at(b4 - 1, g + 1))
                        if causal and kt:
                            of, to = sk[k % 2][0:rows, 0, 0:G * TT], ex[0:rows, g, kt, 0:G * TT]
                        else:
                            of = sk[k % 2][0:rows, :, 0:2 * SP]
                            to = ex[0:rows, g, kt].rearrange("p (a s) -> p a s", a=2)
                        nc.scalar.activation(to, of, ACT.Exp).then_inc(exped.sem, 1)
                    if b5.inside(n):
                        if k == 3:
                            act.wait_ge(h_turned.sem, h_turned.at(b5))
                            nc.scalar.copy(hT[:], onT).then_inc(h_copied.sem, 1)
                        if k >= 4 and not causal:
                            i = k - 4
                            act.wait_ge(stored.of(b5 - 2), stored.at(b5 - 2))
                            act.wait_ge(done.sem, done.at(b5, i + 1))
                            split_high(nc.scalar, parts[:, b5.parity, i, 0], onT, SCALES[i]).then_inc(high.sem, 1)
                        if k == 5 and not causal:
                            act.wait_ge(done.sem, done.at(b5, 3))
                            nc.scalar.copy(res[:, b5.parity, 1], vp).then_inc(finished.sem, 1)
            pipeline(act, n, 5, R, step)

        @block.vector
        def _(dve):
            for e in (maxed, max_high, max_rest, o_copied, recip, o_normed, left):
                e.seed(dve)
            if causal:
                finished.seed(dve)
            dve.wait_ge(const, n_const)
            nc.vector.memset(ks[STACK:AUG], 1.0).then_inc(ready, 1)
            nc.vector.memset(vx[:], 0.0).then_inc(ready, 1)
            dve.wait_ge(ready, 2)
            nc.vector.memset(vx[:, :, :, :, DH:DH + 1], 1.0).then_inc(ready, 1)
            dve.wait_ge(ready, 3)
            if causal:
                nc.vector.tensor_copy(maskb[:], masks[:]).then_inc(ready, 1)
                nc.vector.tensor_copy(identb[:], ident[0:TT, 0:TT]).then_inc(ready, 1)
                nc.vector.tensor_copy(bout2[:, 0], bout[:, 0]).then_inc(ready, 1)
                nc.vector.tensor_copy(bout2[:, 1], bout[:, 0]).then_inc(ready, 1)

            def step(c):
                b2, b3, b4, b5 = c - 2, c - 3, c - 4, c - 5
                for k in range(6):
                    if b3.inside(n) and k == 0:
                        dve.wait_ge(max_turned.sem, max_turned.at(b3))
                        dve.wait_ge(max_in_place.of(b3 - 2), max_in_place.at(b3 - 2))
                        nc.vector.tensor_scalar(mxp[:, b3.parity, 0], mxT, -1.0, None, ALU.mult).then_inc(max_high.sem, 1)
                        dve.wait_ge(max_high.sem, max_high.at(b3))
                        nc.vector.scalar_tensor_tensor(out=mxr[:, b3.parity], in0=mxT, scalar=-1.0,
                                                       in1=mxp[:, b3.parity, 0], op0=ALU.mult,
                                                       op1=ALU.subtract).then_inc(max_rest.sem, 1)
                    if b5.inside(n) and k == 0:
                        dve.wait_ge(summed.sem, summed.at(b5, 3))
                        nc.vector.tensor_copy(ot[:, b5.parity, 2], pv).then_inc(o_copied.sem, 1)
                    if b2.inside(n):
                        for f in (2 * k, 2 * k + 1):
                            qt, h = heads_of(f)
                            width = (TT if qt == 0 else SP) if causal else SEQ
                            dve.wait_ge(scored_q.sem, scored_q.at(b2, f + 1))
                            nc.vector.reduce_max(mx[:, b2.parity, qt, h:h + 2], sq[f % 2][:, :, 0:width],
                                                 AX.X).then_inc(maxed.sem, 1)
                    if b5.inside(n):
                        if k in (1, 2):
                            t = k - 1
                            dve.wait_ge(o_turned.sem, o_turned.at(b5, t + 1))
                            o4 = oT.rearrange("p (h e) -> p h e", e=32)
                            nc.vector.reciprocal(rec[:, t], o4[:, :, DH]).then_inc(recip.sem, 1)
                            dve.wait_ge(recip.sem, recip.at(b5, t + 1))
                            nc.vector.tensor_tensor(on[:, b5.parity, t].rearrange("p (h d) -> p h d", d=DH),
                                                    o4[:, :, 0:DH], rec[:, t].unsqueeze(2).broadcast_to([TT, HEADS, DH]),
                                                    ALU.mult).then_inc(o_normed.sem, 1)
                        if k >= 4 and not causal:
                            dve.wait_ge(high.sem, high.at(b5, k - 3))
                            dve.wait_ge(low.sem, low.at(b5 - 1, k - 3))
                            nc.vector.scalar_tensor_tensor(out=rest[:, k - 4], in0=onT, scalar=SCALES[k - 4],
                                                           in1=parts[:, b5.parity, k - 4, 0], op0=ALU.mult,
                                                           op1=ALU.subtract).then_inc(left.sem, 1)
                        if k == 4 and causal:
                            dve.wait_ge(done.sem, done.at(b5))
                            dve.wait_ge(added.sem, added.at(b5))
                            nc.vector.tensor_tensor(res[:, b5.parity, 0], proj, res[:, b5.parity, 1],
                                                    ALU.add).then_inc(finished.sem, 1)
                    if b4.inside(n) and k in (2, 4):
                        g = k // 2 - 1
                        dve.wait_ge(summed.sem, summed.at(b4, g + 1))
                        nc.vector.tensor_copy(ot[:, b4.parity, g], pv).then_inc(o_copied.sem, 1)
            pipeline(dve, n, 5, R, step)

        @block.tensor
        def _(pe):
            for e in (scored_q, max_turned, scored_k, summed, o_turned, h_turned, done):
                e.seed(pe)
            pe.wait_ge(const, n_const)
            pe.wait_ge(ready, n_ready)

            def query_scores(b, f):
                qt, h = heads_of(f)
                bank = sq[f % 2]
                if f < 2:
                    pe.wait_ge(maxed.sem, maxed.at(b - 1, 11 + f))
                else:
                    pe.wait_ge(maxed.sem, maxed.at(b, f - 1))
                keys = TT * (qt + 1) if causal else SP
                if causal:
                    nc.tensor.matmul(bank[:, :, qt * TT:(qt + 1) * TT], identb[:], mask_of(0, 2), start=True, stop=False,
                                     skip_group_check=True)
                for j in range(2):
                    mm = nc.tensor.matmul(bank[:, j, 0:keys], qs[0:STACK, b.place, h + j, qt * TT:(qt + 1) * TT],
                                          ks[0:STACK, b.place, h + j, 0:keys], start=not causal, stop=True,
                                          skip_group_check=causal)
                mm.then_inc(scored_q.sem, 1)

            def mask_of(i, copies):
                return maskb[:, i:i + 1].broadcast_to([TT, copies, TT])

            def key_scores(b, k):
                g, kt = k // 2, k % 2
                rows = TT - kt
                buf = sk[k % 2]
                if k < 2:
                    pe.wait_ge(exped.sem, exped.at(b - 1, 5 + k))
                else:
                    pe.wait_ge(exped.sem, exped.at(b, k - 1))
                if causal and kt:
                    nc.tensor.matmul(buf[0:rows, 0, 0:G * TT].rearrange("p (h s) -> p h s", h=G),
                                     identb[:, 0:rows], mask_of(1, G), start=True, stop=False, skip_group_check=True)
                    for j in range(G):
                        mm = nc.tensor.matmul(buf[0:rows, 0, j * TT:(j + 1) * TT], ks[:, b.place, G * g + j, TT:TT + rows],
                                              qs[:, b.place, G * g + j, TT:SP], start=False, stop=True, skip_group_check=True)
                else:
                    for a in range(2):
                        if causal:
                            nc.tensor.matmul(buf[0:rows, a, 0:2 * SP].rearrange("p (h s) -> p h s", h=2)[:, :, 0:TT],
                                             identb[:, 0:rows], mask_of(1, 2), start=True, stop=False, skip_group_check=True)
                        for j in range(2):
                            h = G * g + 2 * a + j
                            mm = nc.tensor.matmul(buf[0:rows, a, j * SP:(j + 1) * SP],
                                                  ks[:, b.place, h, kt * TT:kt * TT + rows], qs[:, b.place, h, :],
                                                  start=not causal, stop=True, skip_group_check=causal)
                mm.then_inc(scored_k.sem, 1)

            def value_products(b, g):
                for kt in range(2):
                    pe.wait_ge(exped.sem, exped.at(b, 2 * g + kt + 1))
                    rows = TT - kt
                    for j in range(G):
                        if causal and kt:
                            of, to = ex[0:rows, g, kt, j * TT:(j + 1) * TT], pv[32 * j:32 * j + 32, TT:SP]
                        else:
                            of, to = ex[0:rows, g, kt, j * SP:(j + 1) * SP], pv[32 * j:32 * j + 32, 0:SP]
                        mm = nc.tensor.matmul(to, vx[0:rows, b.place, kt, G * g + j, :], of, start=(kt == 0), stop=(kt == 1),
                                              skip_group_check=causal)
                mm.then_inc(summed.sem, 1)

            def step(c):
                b2, b3, b4, b5 = c - 2, c - 3, c - 4, c - 5
                if b2.inside(n):
                    pe.wait_ge(qk_in_place.of(b2), qk_in_place.at(b2))
                for k in range(6):
                    if k == 0 and b3.inside(n):
                        pe.wait_ge(maxed.sem, maxed.at(b3))
                        if causal:
                            pe.wait_ge(finished.sem, finished.at(c - 6))
                        else:
                            pe.wait_ge(left.sem, left.at(c - 6))
                        for t in range(2):
                            mm = nc.tensor.transpose(mxT[:, t * TT:(t + 1) * TT], mx[:, b3.parity, t], ident[0:TT, 0:TT])
                        mm.then_inc(max_turned.sem, 1)
                    if k == 0 and b5.inside(n):
                        if not causal:
                            pe.wait_ge(finished.sem, finished.at(b5 - 1))
                        pe.wait_ge(o_copied.sem, o_copied.at(b5, 2))
                        value_products(b5, 2)
                    if k == 0 and b4.inside(n):
                        pe.wait_ge(max_in_place.of(b4), max_in_place.at(b4))
                        pe.wait_ge(v_spread.sem, v_spread.at(b4))
                    if b4.inside(n):
                        key_scores(b4, k)
                    if b2.inside(n):
                        query_scores(b2, 2 * k)
                        query_scores(b2, 2 * k + 1)
                    if b5.inside(n):
                        if k in (1, 2):
                            t = k - 1
                            if t:
                                pe.wait_ge(o_normed.sem, o_normed.at(b5, 1))
                            else:
                                pe.wait_ge(o_copied.sem, o_copied.at(b5))
                                if b3.inside(n):
                                    pe.wait_ge(max_rest.sem, max_rest.at(b3))
                            for g in range(NG):
                                mm = nc.tensor.transpose(oT[:, g * 128:(g + 1) * 128], ot[:, b5.parity, g, t * TT:(t + 1) * TT],
                                                         ident[:, :])
                            mm.then_inc(o_turned.sem, 1)
                        if k == 3:
                            pe.wait_ge(o_normed.sem, o_normed.at(b5))
                            if not causal:
                                pe.wait_ge(added.sem, added.at(b5))
                            of = on[:, b5.parity] if causal else res[:, b5.parity, 0]
                            for t in range(2):
                                for h in range(2):
                                    mm = nc.tensor.transpose(onT[:, h, t * TT:(t + 1) * TT],
                                                             of[:, t, h * CH:(h + 1) * CH], ident[0:TT, 0:TT])
                            mm.then_inc(h_turned.sem, 1)
                        if k == 4:
                            pe.wait_ge(h_copied.sem, h_copied.at(b5))
                        if k == 4 and causal:
                            for t in range(2):
                                for h in range(2):
                                    mm = nc.tensor.matmul(proj[:, t], hT[:, h, t * TT:(t + 1) * TT], wout[:, h],
                                                          start=(h == 0), stop=(h == 1))
                            mm.then_inc(done.sem, 1)
                        if k >= 4 and not causal:
                            i = k - 4
                            if i:
                                pe.wait_ge(left.sem, left.at(b5, i))
                            for o in range(2):
                                for h in range(2):
                                    mm = nc.tensor.matmul(onT[:, o], wqkv[:, h, i * D + o * CH:i * D + (o + 1) * CH],
                                                          hT[:, h], start=(h == 0), stop=(h == 1))
                            mm.then_inc(done.sem, 1)
                    if b4.inside(n) and k in (2, 4):
                        g = k // 2 - 1
                        if g:
                            pe.wait_ge(o_copied.sem, o_copied.at(b4, g))
                        else:
                            pe.wait_ge(o_copied.sem, o_copied.at(b4 - 1))
                        value_products(b4, g)
                    if k == 5 and b5.inside(n) and not causal:
                        if b4.inside(n):
                            pe.wait_ge(o_copied.sem, o_copied.at(b4, 2))
                        for t in range(2):
                            for h in range(2):
                                mm = nc.tensor.matmul(vp[:, t], hT[:, h, t * TT:(t + 1) * TT], wqkv[:, h, 2 * D:3 * D],
                                                      start=(h == 0), stop=(h == 1))
                        mm.then_inc(done.sem, 1)
            pipeline(pe, n, 5, R, step)


def route_pass(nc, n, A, scr, y_all):
    R = 4
    with ExitStack() as ctx:
        m = Memory(nc, ctx, R)
        ident = m.sb("r_ident", [128, 128])
        normw = m.sb("r_normw", [TT, D])
        slots = m.sb("r_slots", [SLOTS, D])
        slots2 = m.sb("r_slots2", [SLOTS, D])
        scale = m.sb("r_scale", [SLOTS, 4])
        slotsT = m.sb("r_slotsT", [CH, 2, SLOTS])
        half = m.sb("r_half", [TT, 2])
        hp = m.sb("r_hp", [TT, R, 2, D])
        h2 = m.sb("r_h2", [TT, R, 2, D])
        xn = m.sb("r_xn", [TT, R, 2, D])
        junk = m.sb("r_junk", [TT, 2, D])
        junk2 = m.sb("r_junk2", [TT, 2, D])
        bn = m.sb("r_bn", [TT, 2, 6])
        mv = m.sb("r_mv", [TT, R, 2, 2])
        st = m.sb("r_st", [TT, R, 12, 2])
        ex = m.sb("r_ex", [SLOTS, R, 4])
        xnT = m.sb("r_xnT", [CH, 2, SP])
        lg = m.sb("r_lg", [TT, R, 2, SLOTS])
        cw = m.sb("r_cw", [TT, R, 2, SLOTS])
        dw = m.sb("r_dw", [SLOTS, R, SP])
        cT = m.sb("r_cT", [SLOTS, R, SP])
        dT = m.sb("r_dT", [TT, 2, SLOTS])
        VAR, RSTD, SS, RIN, RMS, NN, NIN, RN, NMAX, DEN, RDEN = range(11)
        xtp = m.ps("r_xtp", [CH, 2, SP])
        lgp = m.ps("r_lgp", [TT, 2, SLOTS])
        lgT = m.ps("r_lgT", [SLOTS, SP])
        cTp = m.ps("r_cTp", [SLOTS, SP])
        dTp = m.ps("r_dTp", [TT, 2, SLOTS])
        yp = m.ps("r_yp", [CH, 2, SLOTS])

        const = m.sem("r_const")
        prep = m.sem("r_prep")
        prep_pow = m.sem("r_prep_pow")
        prep_turned = m.sem("r_prep_turned")
        loaded = m.transfers("r_loaded")
        stats = m.event("r_stats", 2)
        mean_var = m.event("r_mean_var", 2)
        var_eps = m.event("r_var_eps")
        rstd = m.event("r_rstd")
        normed = m.event("r_normed", 2)
        squared = m.event("r_squared", 2)
        ms_eps = m.event("r_ms_eps")
        rms = m.event("r_rms")
        scaled = m.event("r_scaled", 2)
        squared2 = m.event("r_squared2", 2)
        guarded = m.event("r_guarded")
        rnorm = m.event("r_rnorm")
        x_turned = m.event("r_x_turned")
        x_copied = m.event("r_x_copied")
        product = m.event("r_product")
        logits = m.event("r_logits")
        logits_turned = m.event("r_logits_turned")
        maxed = m.event("r_maxed", 2)
        exped = m.event("r_exped", 3)
        recip = m.event("r_recip", 2)
        weighed = m.event("r_weighed", 2)
        w_turned = m.event("r_w_turned", 2)
        w_copied = m.event("r_w_copied", 2)
        y_done = m.event("r_y_done")
        y_copied = m.event("r_y_copied")
        stored = m.transfers("r_stored", 2)
        block = ctx.enter_context(nc.Block())

        @block.sync
        def _(sp):
            for e in (loaded, stored):
                e.seed(sp)
            for to, of in ((ident[:], A["ident"]), (normw[:], A["normw"]), (slots[:], A["slots"]),
                           (scale[:, 0:1], A["scale"])):
                sp.dma_start(to, of).then_inc(const, 16)

            def step(c):
                b = c - 3
                if b.inside(n):
                    sp.wait_ge(normed.sem, normed.at(b))
                    sp.dma_start(scr["h2"][b.number], h2[:, b.place]).then_inc(stored.of(b), 16)
                    sp.wait_ge(w_copied.sem, w_copied.at(b, 1))
                    sp.dma_start(scr["combT"][b.number], cT[:, b.place]).then_inc(stored.of(b), 16)
                if c.inside(n):
                    sp.wait_ge(normed.sem, normed.at(c - 4))
                    sp.dma_start(hp[:, c.place], scr["h_pre"][c.number]).then_inc(loaded.of(c), 16)
            pipeline(sp, n, 3, R, step)
            for i in range(n - R, n):
                sp.wait_ge(stored.of(Image(i // R, i % R, R)), stored.at(Image(i // R, i % R, R)))

        @block.gpsimd
        def _(pool):
            for e in (rstd, rms, rnorm):
                e.seed(pool)
            pool.wait_ge(prep, 4)
            pool.tensor_tensor(scale[:, 2:3], scale[:, 1:2], half[0:SLOTS, 0:1], ALU.pow).then_inc(prep_pow, 1)
            pool.wait_ge(prep_pow, 1)

            def step(c):
                b = c - 1
                if b.inside(n):
                    pool.wait_ge(var_eps.sem, var_eps.at(b))
                    pool.tensor_tensor(st[:, b.place, RSTD], st[:, b.place, VAR], half[:], ALU.pow).then_inc(rstd.sem, 1)
                    pool.wait_ge(ms_eps.sem, ms_eps.at(b))
                    pool.tensor_tensor(st[:, b.place, RMS], st[:, b.place, RIN], half[:], ALU.pow).then_inc(rms.sem, 1)
                    pool.wait_ge(guarded.sem, guarded.at(b))
                    pool.tensor_tensor(st[:, b.place, RN], st[:, b.place, NIN], half[:], ALU.pow).then_inc(rnorm.sem, 1)
            pipeline(pool, n, 3, R, step)

        @block.scalar
        def _(act):
            for e in (squared, squared2, x_copied, exped, w_copied):
                e.seed(act)
            act.wait_ge(prep, 3)

            def step(c):
                b1, b2, b3 = c - 1, c - 2, c - 3
                if b2.inside(n):
                    act.wait_ge(x_turned.sem, x_turned.at(b2))
                    nc.scalar.copy(xnT[:], xtp[:]).then_inc(x_copied.sem, 1)
                if b3.inside(n):
                    act.wait_ge(stored.of(b3 - 4), stored.at(b3 - 4))
                    act.wait_ge(w_turned.sem, w_turned.at(b3, 1))
                    nc.scalar.copy(cT[:, b3.place], cTp[:]).then_inc(w_copied.sem, 1)
                    act.wait_ge(w_turned.sem, w_turned.at(b3, 2))
                    nc.scalar.copy(dT[:], dTp[:]).then_inc(w_copied.sem, 1)
                if b1.inside(n):
                    for t in range(2):
                        act.wait_ge(normed.sem, normed.at(b1, t + 1))
                        nc.scalar.activation(junk[:, t], h2[:, b1.place, t], ACT.Square,
                                             accum_out=st[:, b1.place, SS, t:t + 1]).then_inc(squared.sem, 1)
                if b2.inside(n):
                    act.wait_ge(maxed.sem, maxed.at(b2, 1))
                    for t in range(2):
                        nc.scalar.activation(cw[:, b2.place, t], lg[:, b2.place, t], ACT.Exp, bias=st[:, b2.place, NMAX, t:t + 1],
                                             accum_out=st[:, b2.place, DEN, t:t + 1]).then_inc(exped.sem, 1)
                if b1.inside(n):
                    for t in range(2):
                        act.wait_ge(scaled.sem, scaled.at(b1, t + 1))
                        nc.scalar.activation(junk2[:, t], xn[:, b1.place, t], ACT.Square,
                                             accum_out=st[:, b1.place, NN, t:t + 1]).then_inc(squared2.sem, 1)
                if b2.inside(n):
                    act.wait_ge(maxed.sem, maxed.at(b2, 2))
                    nc.scalar.activation(dw[:, b2.place, 0:SEQ], lgT[:, 0:SEQ], ACT.Exp, bias=ex[:, b2.place, 0:1],
                                         accum_out=ex[:, b2.place, 1:2]).then_inc(exped.sem, 1)
            pipeline(act, n, 3, R, step)

        @block.vector
        def _(dve):
            for e in (stats, mean_var, var_eps, normed, ms_eps, scaled, guarded, logits, maxed, recip, weighed, y_copied):
                e.seed(dve)
            dve.wait_ge(const, 64)
            nc.vector.memset(half[:], -0.5).then_inc(prep, 1)
            nc.vector.memset(dw[:], 0.0).then_inc(prep, 1)
            nc.vector.tensor_tensor_reduce(out=slots2[:], in0=slots[:], in1=slots[:], scale=1.0, scalar=0.0,
                                           op0=ALU.mult, op1=ALU.add, accum_out=scale[:, 3:4]).then_inc(prep, 1)
            dve.wait_ge(prep, 3)
            nc.vector.tensor_scalar(scale[:, 1:2], scale[:, 3:4], 1e-10, None, ALU.max).then_inc(prep, 1)
            dve.wait_ge(prep_pow, 1)
            nc.vector.tensor_scalar(slots2[:], slots[:], scale[:, 2:3], scale[:, 0:1], ALU.mult, ALU.mult).then_inc(prep, 1)
            dve.wait_ge(prep_turned, 1)
            nc.vector.tensor_copy(slotsT[:], xtp[:, :, 0:SLOTS]).then_inc(prep, 1)

            def step(c):
                b1, b2, b3 = c - 1, c - 2, c - 3
                p1, p2, p3 = b1.place, b2.place, b3.place
                if b1.inside(n):
                    dve.wait_ge(loaded.of(b1), loaded.at(b1))
                    for t in range(2):
                        nc.vector.bn_stats(out=bn[:, t], in_=hp[:, p1, t]).then_inc(stats.sem, 1)
                    for t in range(2):
                        dve.wait_ge(stats.sem, stats.at(b1, t + 1))
                        m.hold(dve)
                        nc.vector.bn_aggr(out=mv[:, p1, t], in_=bn[:, t]).then_inc(mean_var.sem, 1)
                    dve.wait_ge(mean_var.sem, mean_var.at(b1))
                    nc.vector.tensor_scalar(st[:, p1, VAR], mv[:, p1, :, 1], LN_EPS, None, ALU.add).then_inc(var_eps.sem, 1)
                if b1.inside(n):
                    dve.wait_ge(rstd.sem, rstd.at(b1))
                    dve.wait_ge(stored.of(b1 - 4), stored.at(b1 - 4))
                    for t in range(2):
                        nc.vector.tensor_scalar(h2[:, p1, t], hp[:, p1, t], mv[:, p1, t, 0:1], st[:, p1, RSTD, t:t + 1],
                                                ALU.subtract, ALU.mult).then_inc(normed.sem, 1)
                if b2.inside(n):
                    dve.wait_ge(product.sem, product.at(b2))
                    dve.wait_ge(rnorm.sem, rnorm.at(b2))
                    nc.vector.tensor_tensor(lg[:, p2], lgp[:], st[:, p2, RN].unsqueeze(2).broadcast_to([TT, 2, SLOTS]),
                                            ALU.mult).then_inc(logits.sem, 1)
                    dve.wait_ge(logits.sem, logits.at(b2))
                    nc.vector.tensor_reduce(st[:, p2, NMAX], lg[:, p2], AX.X, ALU.max, negate=True).then_inc(maxed.sem, 1)
                if b1.inside(n):
                    dve.wait_ge(squared.sem, squared.at(b1))
                    nc.vector.tensor_scalar(st[:, p1, RIN], st[:, p1, SS], 1.0 / D, LN_EPS, ALU.mult, ALU.add).then_inc(ms_eps.sem, 1)
                if b2.inside(n):
                    dve.wait_ge(logits_turned.sem, logits_turned.at(b2))
                    nc.vector.tensor_reduce(ex[:, p2, 0:1], lgT[:, 0:SEQ], AX.X, ALU.max, negate=True).then_inc(maxed.sem, 1)
                if b1.inside(n):
                    dve.wait_ge(rms.sem, rms.at(b1))
                    for t in range(2):
                        dve.wait_ge(normed.sem, normed.at(b1, t + 1))
                        nc.vector.scalar_tensor_tensor(out=xn[:, p1, t], in0=h2[:, p1, t], scalar=st[:, p1, RMS, t:t + 1],
                                                       in1=normw[:], op0=ALU.mult, op1=ALU.mult).then_inc(scaled.sem, 1)
                if b2.inside(n):
                    dve.wait_ge(exped.sem, exped.at(b2, 2))
                    nc.vector.reciprocal(st[:, p2, RDEN], st[:, p2, DEN]).then_inc(recip.sem, 1)
                    dve.wait_ge(recip.sem, recip.at(b2, 1))
                    nc.vector.tensor_tensor(cw[:, p2], cw[:, p2], st[:, p2, RDEN].unsqueeze(2).broadcast_to([TT, 2, SLOTS]),
                                            ALU.mult).then_inc(weighed.sem, 1)
                if b1.inside(n):
                    dve.wait_ge(squared2.sem, squared2.at(b1))
                    nc.vector.tensor_scalar(st[:, p1, NIN], st[:, p1, NN], 1e-10, None, ALU.max).then_inc(guarded.sem, 1)
                if b2.inside(n):
                    dve.wait_ge(exped.sem, exped.at(b2, 3))
                    nc.vector.reciprocal(ex[:, p2, 2:3], ex[:, p2, 1:2]).then_inc(recip.sem, 1)
                    dve.wait_ge(recip.sem, recip.at(b2, 2))
                    nc.vector.tensor_scalar(dw[:, p2, 0:SEQ], dw[:, p2, 0:SEQ], ex[:, p2, 2:3], None, ALU.mult).then_inc(weighed.sem, 1)
                if b3.inside(n):
                    dve.wait_ge(y_done.sem, y_done.at(b3))
                    nc.vector.tensor_copy(y_all[:, :, :, b3.number], yp[:]).then_inc(y_copied.sem, 1)
            pipeline(dve, n, 3, R, step)

        @block.tensor
        def _(pe):
            for e in (x_turned, product, logits_turned, w_turned, y_done):
                e.seed(pe)
            pe.wait_ge(prep, 5)
            pe.wait_ge(const, 64)
            for h in range(2):
                mm = nc.tensor.transpose(xtp[:, h, 0:SLOTS], slots2[:, h * CH:(h + 1) * CH], ident[0:SLOTS, 0:SLOTS])
            mm.then_inc(prep_turned, 1)
            pe.wait_ge(prep, 6)

            def step(c):
                b2, b3 = c - 2, c - 3
                if b2.inside(n):
                    pe.wait_ge(scaled.sem, scaled.at(b2))
                    pe.wait_ge(x_copied.sem, x_copied.at(b2 - 1))
                    for t in range(2):
                        for h in range(2):
                            mm = nc.tensor.transpose(xtp[:, h, t * TT:(t + 1) * TT], xn[:, b2.place, t, h * CH:(h + 1) * CH],
                                                     ident[0:TT, 0:TT])
                    mm.then_inc(x_turned.sem, 1)
                if b3.inside(n):
                    pe.wait_ge(weighed.sem, weighed.at(b3))
                    pe.wait_ge(w_copied.sem, w_copied.at(b3 - 1))
                    m.hold(pe)
                    for t in range(2):
                        mm = nc.tensor.transpose(cTp[:, t * TT:(t + 1) * TT], cw[:, b3.place, t], ident[0:TT, 0:TT])
                    mm.then_inc(w_turned.sem, 1)
                    for t in range(2):
                        mm = nc.tensor.transpose(dTp[:, t], dw[:, b3.place, t * TT:(t + 1) * TT], ident[0:SLOTS, 0:SLOTS])
                    mm.then_inc(w_turned.sem, 1)
                if b2.inside(n):
                    pe.wait_ge(x_copied.sem, x_copied.at(b2))
                    pe.wait_ge(logits.sem, logits.at(b2 - 1))
                    for t in range(2):
                        for h in range(2):
                            mm = nc.tensor.matmul(lgp[:, t], xnT[:, h, t * TT:(t + 1) * TT], slotsT[:, h],
                                                  start=(h == 0), stop=(h == 1))
                    mm.then_inc(product.sem, 1)
                if b3.inside(n):
                    pe.wait_ge(w_copied.sem, w_copied.at(b3))
                    pe.wait_ge(y_copied.sem, y_copied.at(b3 - 1))
                    for h in range(2):
                        for t in range(2):
                            mm = nc.tensor.matmul(yp[:, h], xn[:, b3.place, t, h * CH:(h + 1) * CH], dT[:, t],
                                                  start=(t == 0), stop=(t == 1))
                    mm.then_inc(y_done.sem, 1)
                if b2.inside(n):
                    pe.wait_ge(logits.sem, logits.at(b2))
                    pe.wait_ge(exped.sem, exped.at(b2 - 1))
                    m.hold(pe)
                    for t in range(2):
                        mm = nc.tensor.transpose(lgT[:, t * TT:(t + 1) * TT], lg[:, b2.place, t], ident[0:TT, 0:TT])
                    mm.then_inc(logits_turned.sem, 1)
            pipeline(pe, n, 3, R, step)


def expert_pass(nc, n, A, scr, y_all):
    R = 4
    with ExitStack() as ctx:
        m = Memory(nc, ctx, R)
        w1 = m.sb("x_w1", [CH, R, 2, FF])
        w2 = m.sb("x_w2", [128, R, FC, D])
        b1 = m.sb("x_b1", [128, SLOTS, FC])
        bias = m.sb("x_bias", [128, R, FC])
        ys = m.sb("x_ys", [CH, R, 2, n])
        hid = m.sb("x_hid", [128, 2, FC, n])
        o = m.sb("x_o", [n, R, D])
        hp = [m.ps(f"x_hp{i}", [128, 2, n]) for i in range(FC // 2)]
        op = [m.ps(f"x_op{i}", [n, D]) for i in range(2)]
        const = m.sem("x_const")
        loaded = m.transfers("x_loaded", 2)
        picked = m.event("x_picked", 2)
        hidden = m.event("x_hidden", FC // 2)
        active = m.event("x_active", FC // 2)
        done = m.event("x_done")
        copied = m.event("x_copied")
        stored = m.transfers("x_stored")
        block = ctx.enter_context(nc.Block())

        @block.sync
        def _(sp):
            for e in (loaded, stored):
                e.seed(sp)
            sp.dma_start(b1[:], A["fc1b"]).then_inc(const, 16)

            def step(c):
                if c.inside(SLOTS):
                    sp.wait_ge(done.sem, done.at(c - 4))
                    sp.dma_start(w1[:, c.place], A["fc1"][c.number].rearrange("(c p) f -> p c f", p=CH)).then_inc(loaded.of(c), 16)
                    sp.dma_start(w2[:, c.place], A["fc2"][c.number].rearrange("(k p) d -> p k d", p=128)).then_inc(loaded.of(c), 16)
                b = c - 2
                if b.inside(SLOTS):
                    sp.wait_ge(copied.sem, copied.at(b))
                    sp.dma_start(scr["y2"][:, b.number], o[:, b.place]).then_inc(stored.of(b), 16)
            pipeline(sp, SLOTS, 2, R, step)
            for i in range(SLOTS - R, SLOTS):
                sp.wait_ge(stored.of(Image(i // R, i % R, R)), stored.at(Image(i // R, i % R, R)))

        @block.gpsimd
        def _(pool):
            picked.seed(pool)
            pool.wait_ge(const, 16)

            def step(c):
                if c.inside(SLOTS):
                    pool.wait_ge(hidden.sem, hidden.at(c - 4))
                    pool.wait_ge(active.sem, active.at(c - 4))
                    pool.wait_ge(picked.sem, picked.at(c - 1))
                    m.hold(pool)
                    pool.tensor_copy(ys[:, c.place], y_all[:, :, c.number, :]).then_inc(picked.sem, 1)
                    pool.wait_ge(picked.sem, picked.at(c, 1))
                    m.hold(pool)
                    pool.tensor_copy(bias[:, c.place], b1[:, c.number, :]).then_inc(picked.sem, 1)
            pipeline(pool, SLOTS, 2, R, step)

        @block.scalar
        def _(act):
            active.seed(act)

            def step(c):
                b = c - 1
                if b.inside(SLOTS):
                    act.wait_ge(picked.sem, picked.at(b))
                    act.wait_ge(done.sem, done.at(b - 2))
                    for i in range(FC // 2):
                        act.wait_ge(hidden.sem, hidden.at(b, i + 1))
                        for k in range(2):
                            a = nc.scalar.activation(hid[:, b.parity, 2 * i + k], hp[i][:, k], ACT.Gelu,
                                                     bias=bias[:, b.place, 2 * i + k:2 * i + k + 1])
                        a.then_inc(active.sem, 1)
            pipeline(act, SLOTS, 2, R, step)

        @block.vector
        def _(dve):
            copied.seed(dve)

            def step(c):
                b = c - 2
                if b.inside(SLOTS):
                    dve.wait_ge(done.sem, done.at(b))
                    dve.wait_ge(stored.of(b - 4), stored.at(b - 4))
                    nc.vector.tensor_copy(o[:, b.place], op[b.parity][:]).then_inc(copied.sem, 1)
            pipeline(dve, SLOTS, 2, R, step)

        @block.tensor
        def _(pe):
            for e in (hidden, done):
                e.seed(pe)

            def step(c):
                b = c - 1
                if b.inside(SLOTS):
                    pe.wait_ge(loaded.of(b), loaded.at(b))
                    pe.wait_ge(picked.sem, picked.at(b, 1))
                    for i in range(FC // 2):
                        pe.wait_ge(active.sem, active.at(b - 1, i + 1))
                        for k in range(2):
                            f = 2 * i + k
                            for h in range(2):
                                mm = nc.tensor.matmul(hp[i][:, k], w1[:, b.place, h, f * 128:(f + 1) * 128],
                                                      ys[:, b.place, h], start=(h == 0), stop=(h == 1))
                        mm.then_inc(hidden.sem, 1)
                b = c - 2
                if b.inside(SLOTS):
                    pe.wait_ge(active.sem, active.at(b))
                    pe.wait_ge(copied.sem, copied.at(b - 2))
                    for k in range(FC):
                        mm = nc.tensor.matmul(op[b.parity][:], hid[:, b.parity, k], w2[:, b.place, k],
                                              start=(k == 0), stop=(k == FC - 1))
                    mm.then_inc(done.sem, 1)
            pipeline(pe, SLOTS, 2, R, step)


def combine_pass(nc, n, A, scr, out):
    R = 4
    with ExitStack() as ctx:
        m = Memory(nc, ctx, R)
        b2 = m.sb("o_b2", [SLOTS, D])
        y = m.sb("o_y", [SLOTS, R, D])
        yb = m.sb("o_yb", [SLOTS, R, D])
        cT = m.sb("o_cT", [SLOTS, R, SP])
        h2 = m.sb("o_h2", [TT, R, 2, D])
        z = m.sb("o_z", [TT, R, 2, D])
        res = m.sb("o_res", [TT, R, 2, D])
        bn = m.sb("o_bn", [TT, 2, 6])
        mv = m.sb("o_mv", [TT, R, 2, 2])
        st = m.sb("o_st", [TT, R, 2, 2])
        half = m.sb("o_half", [TT, 2])
        zp = [m.ps(f"o_zp{i}", [TT, 2, D]) for i in range(2)]
        const = m.sem("o_const")
        ready = m.sem("o_ready")
        loaded = m.transfers("o_loaded", 3)
        biased = m.event("o_biased")
        mixed = m.event("o_mixed")
        summed = m.event("o_summed")
        stats = m.event("o_stats", 2)
        mean_var = m.event("o_mean_var", 2)
        var_eps = m.event("o_var_eps")
        rstd = m.event("o_rstd")
        normed = m.event("o_normed", 2)
        stored = m.transfers("o_stored", 2)
        block = ctx.enter_context(nc.Block())

        @block.sync
        def _(sp):
            for e in (loaded, stored):
                e.seed(sp)
            sp.dma_start(b2[:], A["fc2b"]).then_inc(const, 16)

            def step(c):
                if c.inside(n):
                    sp.wait_ge(mixed.sem, mixed.at(c - 4))
                    sp.wait_ge(summed.sem, summed.at(c - 4))
                    sp.dma_start(y[:, c.place], scr["y2"][c.number]).then_inc(loaded.of(c), 16)
                    sp.dma_start(cT[:, c.place], scr["combT"][c.number]).then_inc(loaded.of(c), 16)
                    sp.dma_start(h2[:, c.place], scr["h2"][c.number]).then_inc(loaded.of(c), 16)
                b = c - 3
                if b.inside(n):
                    for t in range(2):
                        sp.wait_ge(normed.sem, normed.at(b, t + 1))
                        sp.dma_start(out[b.number, t * TT:min(SEQ, (t + 1) * TT)],
                                     res[0:TT - t, b.place, t]).then_inc(stored.of(b), 16)
            pipeline(sp, n, 3, R, step)
            for i in range(n - R, n):
                sp.wait_ge(stored.of(Image(i // R, i % R, R)), stored.at(Image(i // R, i % R, R)))

        @block.gpsimd
        def _(pool):
            for e in (biased, rstd):
                e.seed(pool)
            pool.wait_ge(const, 16)
            pool.wait_ge(ready, 1)

            def step(c):
                b = c - 1
                if b.inside(n):
                    pool.wait_ge(loaded.of(b), loaded.at(b))
                    pool.wait_ge(mixed.sem, mixed.at(b - 4))
                    if (c - 3).inside(n):
                        pool.wait_ge(rstd.sem, rstd.at(c - 3))
                    pool.tensor_tensor(yb[:, b.place], y[:, b.place], b2[:], ALU.add).then_inc(biased.sem, 1)
                b = c - 2
                if b.inside(n):
                    pool.wait_ge(var_eps.sem, var_eps.at(b))
                    if (c - 1).inside(n):
                        pool.wait_ge(biased.sem, biased.at(c - 1))
                    pool.tensor_tensor(st[:, b.place, 1], st[:, b.place, 0], half[:], ALU.pow).then_inc(rstd.sem, 1)
            pipeline(pool, n, 3, R, step)

        @block.vector
        def _(dve):
            for e in (summed, stats, mean_var, var_eps, normed):
                e.seed(dve)
            nc.vector.memset(half[:], -0.5).then_inc(ready, 1)

            def step(c):
                b = c - 2
                if b.inside(n):
                    dve.wait_ge(mixed.sem, mixed.at(b))
                    dve.wait_ge(loaded.of(b), loaded.at(b))
                    nc.vector.tensor_tensor(z[:, b.place], zp[b.parity][:], h2[:, b.place], ALU.add).then_inc(summed.sem, 1)
                    dve.wait_ge(summed.sem, summed.at(b))
                    for t in range(2):
                        nc.vector.bn_stats(out=bn[:, t], in_=z[:, b.place, t]).then_inc(stats.sem, 1)
                    for t in range(2):
                        dve.wait_ge(stats.sem, stats.at(b, t + 1))
                        m.hold(dve)
                        nc.vector.bn_aggr(out=mv[:, b.place, t], in_=bn[:, t]).then_inc(mean_var.sem, 1)
                    dve.wait_ge(mean_var.sem, mean_var.at(b))
                    nc.vector.tensor_scalar(st[:, b.place, 0], mv[:, b.place, :, 1], LN_EPS, None, ALU.add).then_inc(var_eps.sem, 1)
                b = c - 3
                if b.inside(n):
                    dve.wait_ge(rstd.sem, rstd.at(b))
                    dve.wait_ge(stored.of(b - 4), stored.at(b - 4))
                    for t in range(2):
                        nc.vector.tensor_scalar(res[:, b.place, t], z[:, b.place, t], mv[:, b.place, t, 0:1],
                                                st[:, b.place, 1, t:t + 1], ALU.subtract, ALU.mult).then_inc(normed.sem, 1)
            pipeline(dve, n, 3, R, step)

        @block.tensor
        def _(pe):
            mixed.seed(pe)

            def step(c):
                b = c - 1
                if b.inside(n):
                    pe.wait_ge(biased.sem, biased.at(b))
                    pe.wait_ge(loaded.of(b), loaded.at(b))
                    pe.wait_ge(summed.sem, summed.at(b - 2))
                    for t in range(2):
                        mm = nc.tensor.matmul(zp[b.parity][:, t], cT[:, b.place, t * TT:(t + 1) * TT], yb[:, b.place],
                                              start=True, stop=True)
                    mm.then_inc(mixed.sem, 1)
            pipeline(pe, n, 3, R, step)


def route_and_experts(nc, n, A, scr):
    with nc.sbuf_tensor("y_all", [CH, 2, SLOTS, n], F32) as y_all:
        route_pass(nc, n, A, scr, y_all)
        expert_pass(nc, n, A, scr, y_all)


def scratch(nc, n, kind="Internal"):
    shapes = {"tv1": ([n, TT, 2, 2, D], F32), "tv2": ([n, TT, 2, 2, D], F32),
              "qk1": ([n, 2, PARTS, D, SP], BF16), "qk2": ([n, 2, PARTS, D, SP], BF16),
              "max1": ([n, PARTS, HEADS, SP], BF16), "max2": ([n, PARTS, HEADS, SP], BF16),
              "h_pre": ([n, TT, 2, D], F32), "h2": ([n, TT, 2, D], F32),
              "combT": ([n, SLOTS, SP], F32), "y2": ([n, SLOTS, D], F32)}
    return {k: nc.dram_tensor(f"scr_{k}", s, t, kind=kind).ap() for k, (s, t) in shapes.items()}


def position_table():
    i = np.arange(SEQ, dtype=np.float32)[:, None]
    j = np.arange(D, dtype=np.float32)[None, :]
    even = np.power(np.float32(10000.0), j / D).astype(np.float32)
    odd = np.power(np.float32(10000.0), (j - 1.0) / D).astype(np.float32)
    table = np.zeros((SP, D), np.float32)
    table[:SEQ] = np.where(np.arange(D)[None, :] % 2 == 0, np.sin(i / even), np.cos(i / odd))
    return table


def lay_out(x, v):
    def padded(a):
        out = np.zeros((SP, D), np.float32)
        out[:SEQ] = a
        return out

    rowb = np.zeros((SP, D), np.float32)
    rowb[0] = v["L0_tok_class_token"][0]
    rowb[1:SEQ] = v["L0_tok_b_map"][None]
    wqkv1 = np.zeros((CH + 1, 3, 2, CH), np.float32)
    for i, (w, b) in enumerate((("Wq", "bq"), ("Wk", "bk"), ("Wv", "bv"))):
        for h in range(HEADS):
            c, r = h // HC, (h % HC) * DH
            wqkv1[r:r + DH, i, c, r:r + DH] = v["L0_tok_" + w][h].T
            wqkv1[CH, i, c, r:r + DH] = v["L0_tok_" + b][h]
    above = np.where(np.arange(TT)[None, :] > np.arange(TT)[:, None], np.float32(MASKED), np.float32(0))
    return {
        "x": np.ascontiguousarray(x).reshape(x.shape[0], PATCHES, INPUT),
        "wmapT": np.ascontiguousarray(v["L0_tok_W_map"].T),
        "wqkv1": wqkv1,
        "pos": position_table(), "rowb": rowb,
        "lnw": padded(v["L0_tok_ln_w"]), "lnb": padded(v["L0_tok_ln_b"]),
        "ident": np.eye(128, dtype=np.float32),
        "above": above, "aboveT": np.ascontiguousarray(above.T),
        "wqkv2": v["L0_attn_W_qkv"], "wout": v["L0_attn_W_out"],
        "bout": np.ascontiguousarray(np.broadcast_to(v["L0_attn_b_out"], (TT, D))),
        "slots": v["L0_ffn_slots"], "scale": np.ascontiguousarray(v["L0_ffn_scale"][:, None]),
        "normw": np.ascontiguousarray(np.broadcast_to(v["L0_ffn_norm_weight"], (TT, D))),
        "fc1": v["L0_ffn_fc1_weight"], "fc2": v["L0_ffn_fc2_weight"],
        "fc1b": np.ascontiguousarray(v["L0_ffn_fc1_bias"].reshape(SLOTS, FC, 128).transpose(2, 0, 1)),
        "fc2b": v["L0_ffn_fc2_bias"],
    }


def build(nc, A, n, out):
    scr = scratch(nc, n)
    embed_pass(nc, n, A, scr)
    attend_pass(nc, n, A, scr, causal=False)
    attend_pass(nc, n, A, scr, causal=True)
    route_and_experts(nc, n, A, scr)
    combine_pass(nc, n, A, scr, out)


def kernel(x, **weights):
    import concourse.bacc as bacc
    from concourse.bass_utils import run_bass_kernel_spmd

    arrays = lay_out(np.asarray(x), {k: np.asarray(a) for k, a in weights.items()})
    n = arrays["x"].shape[0]
    nc = bacc.Bacc("TRN2", target_bir_lowering=False, num_devices=1)
    A = {k: nc.dram_tensor(f"in_{k}", list(a.shape), mybir.dt.from_np(a.dtype), kind="ExternalInput").ap()
         for k, a in arrays.items()}
    out = nc.dram_tensor("out", [n, SEQ, D], F32, kind="ExternalOutput").ap()
    build(nc, A, n, out)
    r = run_bass_kernel_spmd(nc, [{f"in_{k}": a for k, a in arrays.items()}], core_ids=[0])
    return r.results[0]["out"]
```

```python
from contextlib import ExitStack

import concourse.bass as bass
import numpy as np
from concourse import mybir

F32 = mybir.dt.float32
BF16 = mybir.dt.bfloat16
ALU = mybir.AluOpType
ACT = mybir.ActivationFunctionType
AX = mybir.AxisListType

D = 192
HEADS = 12
DH = D // HEADS
CH = D // 2
HC = HEADS // 2
SEQ = 197
TT = 99
SP = 2 * TT
PATCHES = SEQ - 1
PT = PATCHES // 2
INPUT = 768
KC = INPUT // 128
SLOTS = 64
FF = 768
FC = FF // 128
PARTS = 3
GROUPS = PARTS * (PARTS + 1) // 2
STACK = GROUPS * DH
AUG = STACK + PARTS
SCALES = (0.25, 1.0)
LN_EPS = 1e-5
READY1 = 8
MASKED = -3e38
G = 4
NG = HEADS // G


class Image:

    def __init__(self, turn, place, R):
        self.turn, self.place, self.R = turn, place, R

    def __sub__(self, s):
        at = self.place - s
        return Image(self.turn + at // self.R, at % self.R, self.R)

    @property
    def number(self):
        return self.turn * self.R + self.place

    @property
    def parity(self):
        return self.place % 2

    def inside(self, n):
        return not isinstance(self.turn, int) or 0 <= self.number < n


class Event:

    def __init__(self, sem, n, R):
        self.sem, self.n, self.R = sem, n, R

    def seed(self, eng):
        eng.sem_inc(self.sem, self.R * self.n)

    def at(self, image, k=None):
        return image.number * self.n + (self.R * self.n + (self.n if k is None else k))


class Transfers:

    def __init__(self, sems, n):
        self.sems, self.n = sems, 16 * n

    def seed(self, eng):
        for sem in self.sems:
            eng.sem_inc(sem, self.n)

    def of(self, image):
        return self.sems[image.place]

    def at(self, image):
        return (image.turn + 2) * self.n


def pipeline(eng, n, depth, R, step):
    head = depth + (n - depth) % R
    for c in range(head):
        step(Image(c // R, c % R, R))
    if n > head:
        with eng.Fori(0, (n - head) // R) as j:
            for c in range(head, head + R):
                step(Image(j + c // R, c % R, R))
    for c in range(n, n + depth):
        step(Image(c // R, c % R, R))


class Memory:

    def __init__(self, nc, ctx, R):
        self.nc, self.ctx, self.R, self.sems = nc, ctx, R, []
        self.held = self.sem(f"held{nc.next_id()}")
        ctx.callback(self.release)

    def sb(self, name, shape, dt=F32):
        return self.ctx.enter_context(self.nc.sbuf_tensor(name, shape, dt))

    def ps(self, name, shape, dt=F32):
        return self.ctx.enter_context(self.nc.psum_tensor(name, shape, dt))

    def sem(self, name):
        self.sems.append(self.nc.alloc_semaphore(name=name))
        return self.sems[-1]

    def hold(self, eng):
        eng.sem_inc(self.held, 1)

    def release(self):
        self.nc.clear_and_free_semaphores(self.sems)
        self.nc.all_engine_barrier()

    def event(self, name, n=1):
        return Event(self.sem(name), n, self.R)

    def transfers(self, name, n=1):
        return Transfers([self.sem(f"{name}{i}") for i in range(self.R)], n)


def place_of(i, part):
    return PARTS - 1 - part if i else part


def split_high(act, parts, psum, scale):
    return act.activation(parts, psum, ACT.Copy, scale=scale)


def embed_pass(nc, n, A, scr):
    R = 4
    with ExitStack() as ctx:
        m = Memory(nc, ctx, R)
        patches = m.sb("e_patches", [PT, R, 2, INPUT])
        wmap = m.sb("e_wmap", [128, KC, D])
        wqkv = m.sb("e_wqkv", [CH + 1, 3, 2, CH])
        posb = m.sb("e_posb", [TT, 2, D])
        rowb = m.sb("e_rowb", [TT, 2, D])
        lnw = m.sb("e_lnw", [TT, 2, D])
        lnb = m.sb("e_lnb", [TT, 2, D])
        ident = m.sb("e_ident", [128, 128])
        cmean = m.sb("e_cmean", [TT, TT])
        cvar = m.sb("e_cvar", [TT, 2, TT])
        eps = m.sb("e_eps", [TT, 1])
        ptT = m.sb("e_ptT", [128, 2, KC, SP])
        tv = m.sb("e_tv", [TT, R, 2, 2, D])
        xc = m.sb("e_xc", [TT, 2, 2, D])
        xn = m.sb("e_xn", [TT, 2, 2, D])
        junk = m.sb("e_junk", [TT, 2, D])
        xT = m.sb("e_xT", [CH + 1, 2, 2, SP])
        rest = m.sb("e_rest", [CH, 2, 2, 2, SP])
        parts = m.sb("e_parts", [CH, R, 2, 2, PARTS, SP], BF16)
        st = m.sb("e_st", [TT, 2, 8])
        tpp = [m.ps(f"e_tp{i}", [128, 2, PATCHES]) for i in range(3)]
        tokp = m.ps("e_tokp", [TT, 2, D])
        statp = m.ps("e_statp", [TT, 2])
        xtp = m.ps("e_xtp", [128, 512])
        qp = m.ps("e_qp", [CH, 2, SP])
        kp = m.ps("e_kp", [CH, 2, SP])
        vp = xtp[0:TT, 0:2 * D].rearrange("p (t d) -> p t d", t=2)
        xtv = xtp[0:CH, 0:2 * SP].rearrange("p (c s) -> p c s", c=2)

        const = m.sem("e_const")
        ready = m.sem("e_ready")
        loaded = m.transfers("e_loaded")
        turned = m.event("e_turned", 3)
        turned_a = m.event("e_turned_a", 2)
        turned_v = m.event("e_turned_v", 1)
        embedded = m.event("e_embedded")
        tokens = m.event("e_tokens")
        mean_p = m.event("e_mean_p")
        mean_s = m.event("e_mean_s")
        squares = m.event("e_squares", 2)
        var_p = m.event("e_var_p")
        std = m.event("e_std")
        rstd = m.event("e_rstd")
        centred = m.event("e_centred")
        normed = m.event("e_normed")
        x_turned = m.event("e_x_turned")
        x_copied = m.event("e_x_copied")
        q_done = m.event("e_q_done")
        k_done = m.event("e_k_done")
        v_done = m.event("e_v_done")
        v_copied = m.event("e_v_copied")
        high = m.event("e_high", 2)
        left = m.event("e_left", 2)
        middle = m.event("e_middle", 2)
        low = m.event("e_low", 2)
        stored = m.transfers("e_stored", 2)

        block = ctx.enter_context(nc.Block())

        @block.sync
        def _(sp):
            loads = [(wmap[:], A["wmapT"].rearrange("(k p) d -> p k d", p=128)), (wqkv[:], A["wqkv1"]),
                     (posb[:], A["pos"].rearrange("(t p) d -> p t d", p=TT)),
                     (rowb[:], A["rowb"].rearrange("(t p) d -> p t d", p=TT)),
                     (lnw[:], A["lnw"].rearrange("(t p) d -> p t d", p=TT)),
                     (lnb[:], A["lnb"].rearrange("(t p) d -> p t d", p=TT)), (ident[:], A["ident"])]
            for e in (loaded, stored):
                e.seed(sp)
            for to, of in loads:
                sp.dma_start(to, of).then_inc(const, 16)

            def step(c):
                if c.inside(n):
                    sp.wait_ge(turned.sem, turned.at(c - 4))
                    sp.dma_start(patches[:, c.place], A["x"][c.number].rearrange("(t p) i -> p t i", t=2)).then_inc(loaded.of(c), 16)
                b = c - 3
                if b.inside(n):
                    sp.wait_ge(v_copied.sem, v_copied.at(b))
                    sp.dma_start(scr["tv1"][b.number], tv[:, b.place]).then_inc(stored.of(b), 16)
                    sp.wait_ge(low.sem, low.at(b))
                    sp.dma_start(scr["qk1"][b.number].rearrange("i c a p s -> p (i c a) s"),
                                 parts[:, b.place].rearrange("p i c a s -> p (i c a) s")).then_inc(stored.of(b), 16)
            pipeline(sp, n, 3, R, step)
            for i in range(n - R, n):
                sp.wait_ge(stored.of(Image(i // R, i % R, R)), stored.at(Image(i // R, i % R, R)))

        @block.gpsimd
        def _(pool):
            for e in (middle, low):
                e.seed(pool)

            def step(c):
                c = c - 1
                u = c.parity
                b = c - 2
                if b.inside(n):
                    for i in range(2):
                        pool.wait_ge(left.sem, left.at(b, i + 1))
                        pool.wait_ge(stored.of(b - 4), stored.at(b - 4))
                        m.hold(pool)
                        pool.tensor_copy(parts[:, b.place, i, :, place_of(i, 1)], rest[:, u, i]).then_inc(middle.sem, 1)
                        pool.wait_ge(middle.sem, middle.at(b, i + 1))
                        pool.tensor_tensor(parts[:, b.place, i, :, place_of(i, 2)], rest[:, u, i], parts[:, b.place, i, :, place_of(i, 1)],
                                           ALU.subtract).then_inc(low.sem, 1)
            pipeline(pool, n, 3, R, step)

        @block.scalar
        def _(act):
            for e in (turned_a, squares, std, x_copied, high):
                e.seed(act)
            act.wait_ge(const, 16 * 7)
            act.wait_ge(ready, READY1)

            def step(c):
                c = c - 1
                u = c.parity
                b = c - 2
                if b.inside(n):
                    act.wait_ge(x_turned.sem, x_turned.at(b))
                    nc.scalar.copy(xT[0:CH, u], xtv).then_inc(x_copied.sem, 1)
                if c.inside(n):
                    for i in range(2):
                        act.wait_ge(turned.sem, turned.at(c, i + 1))
                        nc.scalar.copy(ptT[:, u, 2 * i:2 * i + 2, 1:1 + PATCHES], tpp[i][:]).then_inc(turned_a.sem, 1)
                b = c - 1
                w = 1 - u
                if b.inside(n):
                    act.wait_ge(mean_s.sem, mean_s.at(b))
                    for t in range(2):
                        nc.scalar.activation(junk[:, t], tv[:, b.place, 0, t], ACT.Square, bias=st[:, w, 1:2],
                                             accum_out=st[:, w, 2 + t:3 + t]).then_inc(squares.sem, 1)
                b = c - 2
                if b.inside(n):
                    act.wait_ge(stored.of(b - 4), stored.at(b - 4))
                    for i, (done, p) in enumerate(((q_done, qp), (k_done, kp))):
                        act.wait_ge(done.sem, done.at(b))
                        split_high(nc.scalar, parts[:, b.place, i, :, place_of(i, 0)], p[:], SCALES[i]).then_inc(high.sem, 1)
                b = c - 1
                if b.inside(n):
                    act.wait_ge(var_p.sem, var_p.at(b))
                    nc.scalar.activation(st[:, w, 4:5], statp[:, 1:2], ACT.Sqrt, bias=eps[:, 0:1]).then_inc(std.sem, 1)
            pipeline(act, n, 3, R, step)

        @block.vector
        def _(dve):
            for e in (turned_v, tokens, mean_s, rstd, centred, normed, v_copied, left):
                e.seed(dve)
            dve.wait_ge(const, 16 * 7)
            nc.vector.memset(ptT[:], 0.0).then_inc(ready, 1)
            nc.vector.memset(xT[CH:CH + 1], 1.0).then_inc(ready, 1)
            nc.vector.memset(cmean[:], -1.0 / (SEQ * D)).then_inc(ready, 1)
            nc.vector.memset(cvar[:], 0.0).then_inc(ready, 1)
            nc.vector.memset(eps[:], LN_EPS).then_inc(ready, 1)
            nc.vector.tensor_tensor(posb[:], posb[:], rowb[:], ALU.add).then_inc(ready, 1)
            dve.wait_ge(ready, READY1 - 2)
            nc.vector.tensor_scalar(cvar[0:TT, 0], cvar[0:TT, 0], 1.0 / (SEQ * D), None, ALU.add).then_inc(ready, 1)
            nc.vector.tensor_scalar(cvar[0:TT - 1, 1], cvar[0:TT - 1, 1], 1.0 / (SEQ * D), None, ALU.add).then_inc(ready, 1)
            dve.wait_ge(ready, READY1)

            def step(c):
                c = c - 1
                u = c.parity
                w = 1 - u
                b = c - 1
                if b.inside(n):
                    dve.wait_ge(embedded.sem, embedded.at(b))
                    dve.wait_ge(stored.of(b - 4), stored.at(b - 4))
                    nc.vector.scalar_tensor_tensor(out=tv[:, b.place, 0], in0=tokp[:], scalar=1.0, in1=posb[:],
                                                   op0=ALU.mult, op1=ALU.add,
                                                   accum_out=st[:, w, 0:1]).then_inc(tokens.sem, 1)
                if c.inside(n):
                    dve.wait_ge(turned.sem, turned.at(c, 3))
                    nc.vector.tensor_copy(ptT[:, u, 4:6, 1:1 + PATCHES], tpp[2][:]).then_inc(turned_v.sem, 1)
                if b.inside(n):
                    dve.wait_ge(mean_p.sem, mean_p.at(b))
                    nc.vector.tensor_copy(st[:, w, 1:2], statp[:, 0:1]).then_inc(mean_s.sem, 1)
                    dve.wait_ge(mean_s.sem, mean_s.at(b))
                    nc.vector.scalar_tensor_tensor(out=xc[:, w], in0=tv[:, b.place, 0], scalar=st[:, w, 1:2], in1=lnw[:],
                                                   op0=ALU.add, op1=ALU.mult).then_inc(centred.sem, 1)
                b2 = c - 2
                if b2.inside(n):
                    for i, (done, p) in enumerate(((q_done, qp), (k_done, kp))):
                        dve.wait_ge(high.sem, high.at(b2, i + 1))
                        dve.wait_ge(low.sem, low.at(b2 - 2, i + 1))
                        nc.vector.scalar_tensor_tensor(out=rest[:, u, i], in0=p[:], scalar=SCALES[i],
                                                       in1=parts[:, b2.place, i, :, place_of(i, 0)], op0=ALU.mult,
                                                       op1=ALU.subtract).then_inc(left.sem, 1)
                    dve.wait_ge(v_done.sem, v_done.at(b2))
                    nc.vector.tensor_copy(tv[:, b2.place, 1], vp).then_inc(v_copied.sem, 1)
                if b.inside(n):
                    dve.wait_ge(std.sem, std.at(b))
                    nc.vector.reciprocal(st[:, w, 5:6], st[:, w, 4:5]).then_inc(rstd.sem, 1)
                    dve.wait_ge(rstd.sem, rstd.at(b))
                    dve.wait_ge(centred.sem, centred.at(b))
                    nc.vector.scalar_tensor_tensor(out=xn[:, w], in0=xc[:, w], scalar=st[:, w, 5:6], in1=lnb[:],
                                                   op0=ALU.mult, op1=ALU.add).then_inc(normed.sem, 1)
            pipeline(dve, n, 3, R, step)

        @block.tensor
        def _(pe):
            for e in (turned, embedded, mean_p, var_p, x_turned, q_done, k_done, v_done):
                e.seed(pe)
            pe.wait_ge(const, 16 * 7)
            pe.wait_ge(ready, READY1)

            def step(c):
                c = c - 1
                u = c.parity
                w = 1 - u
                b1, b2 = c - 1, c - 2
                if b1.inside(n):
                    pe.wait_ge(turned_a.sem, turned_a.at(b1))
                    pe.wait_ge(turned_v.sem, turned_v.at(b1))
                    pe.wait_ge(tokens.sem, tokens.at(b1 - 1))
                    for t in range(2):
                        for k in range(KC):
                            mm = nc.tensor.matmul(tokp[:, t], ptT[:, w, k, t * TT:(t + 1) * TT], wmap[:, k],
                                                  start=(k == 0), stop=(k == KC - 1))
                    mm.then_inc(embedded.sem, 1)
                if b2.inside(n):
                    pe.wait_ge(normed.sem, normed.at(b2))
                    pe.wait_ge(v_copied.sem, v_copied.at(b2 - 1))
                    for t in range(2):
                        for h in range(2):
                            mm = nc.tensor.transpose(xtv[:, h, t * TT:(t + 1) * TT],
                                                     xn[:, u, t, h * CH:(h + 1) * CH], ident[0:TT, 0:TT])
                    mm.then_inc(x_turned.sem, 1)
                if c.inside(n):
                    pe.wait_ge(loaded.of(c), loaded.at(c))
                    for i in range(3):
                        if i < 2:
                            pe.wait_ge(turned_a.sem, turned_a.at(c - 1, i + 1))
                        else:
                            pe.wait_ge(turned_v.sem, turned_v.at(c - 1))
                        for k in range(2):
                            for t in range(2):
                                mm = nc.tensor.transpose(tpp[i][:, k, t * PT:(t + 1) * PT],
                                                         patches[:, c.place, t, (2 * i + k) * 128:(2 * i + k + 1) * 128],
                                                         ident[0:PT, 0:PT])
                        mm.then_inc(turned.sem, 1)
                if b1.inside(n):
                    pe.wait_ge(tokens.sem, tokens.at(b1))
                    pe.wait_ge(std.sem, std.at(b1 - 1))
                    nc.tensor.matmul(statp[:, 0:1], cmean[:], st[:, w, 0:1], start=True, stop=True).then_inc(mean_p.sem, 1)
                if b2.inside(n):
                    pe.wait_ge(x_copied.sem, x_copied.at(b2))
                    for i, (done, p) in enumerate(((q_done, qp), (k_done, kp))):
                        pe.wait_ge(left.sem, left.at(b2 - 1, i + 1))
                        for h in range(2):
                            mm = nc.tensor.matmul(p[:, h], wqkv[:, i, h], xT[:, u, h], start=True, stop=True)
                        mm.then_inc(done.sem, 1)
                    for t in range(2):
                        for h in range(2):
                            mm = nc.tensor.matmul(vp[:, t, h * CH:(h + 1) * CH], xT[:, u, h, t * TT:(t + 1) * TT],
                                                  wqkv[:, 2, h], start=True, stop=True)
                    mm.then_inc(v_done.sem, 1)
                if b1.inside(n):
                    pe.wait_ge(squares.sem, squares.at(b1))
                    for t in range(2):
                        mm = nc.tensor.matmul(statp[:, 1:2], cvar[:, t], st[:, w, 2 + t:3 + t],
                                              start=(t == 0), stop=(t == 1))
                    mm.then_inc(var_p.sem, 1)
            pipeline(pe, n, 3, R, step)


def attend_pass(nc, n, A, scr, causal):
    R = 4
    X = "c_" if causal else "a_"
    qk_in, tv_in = (scr["qk2"], scr["tv2"]) if causal else (scr["qk1"], scr["tv1"])
    with ExitStack() as ctx:
        m = Memory(nc, ctx, R)
        qs = m.sb(X + "qs", [AUG, R, HEADS, SP], BF16)
        ks = m.sb(X + "ks", [AUG, R, HEADS, SP], BF16)
        tv = m.sb(X + "tv", [TT, R, 2, 2, D])
        vx = m.sb(X + "vx", [TT, R, 2, HEADS, 32])
        mx = m.sb(X + "mx", [TT, 2, 2, HEADS])
        mxp = m.sb(X + "mxp", [HEADS, 2, PARTS, SP], BF16)
        mxr = m.sb(X + "mxr", [HEADS, 2, SP])
        ex = m.sb(X + "ex", [TT, NG, 2, G * SP])
        ot = m.sb(X + "ot", [128, 2, NG, SP])
        rec = m.sb(X + "rec", [TT, 2, HEADS])
        on = m.sb(X + "on", [TT, 2, 2, D])
        hT = m.sb(X + "hT", [CH, 2, SP])
        ident = m.sb(X + "ident", [128, 128])
        res = m.sb(X + "res", [TT, 2, 2, 2, D])
        if causal:
            wout = m.sb(X + "wout", [CH, 2, D])
            bout = m.sb(X + "bout", [TT, 1, D])
            bout2 = m.sb(X + "bout2", [TT, 2, D])
            masks = m.sb(X + "masks", [TT, 2, TT])
            maskb = m.sb(X + "maskb", [TT, 2, TT], BF16)
            identb = m.sb(X + "identb", [TT, TT], BF16)
        else:
            wqkv = m.sb(X + "wqkv", [CH, 2, 3 * D])
            rest = m.sb(X + "rest", [CH, 2, 2, SP])
            parts = m.sb(X + "parts", [CH, 2, 2, 2, PARTS, SP], BF16)

        sq = [m.ps(f"{X}sq{i}", [TT, 2, SP]) for i in range(2)]
        sk = [m.ps(f"{X}sk{i}", [TT, 2, 512]) for i in range(2)]
        pvp = m.ps(X + "pvp", [128, 512])
        work = m.ps(X + "work", [128, 512])
        pv = pvp[:, 0:SP]
        vp = pvp[0:TT, 0:2 * D].rearrange("p (t d) -> p t d", t=2)
        mxT = work[0:HEADS, 0:SP]
        oT = work[0:TT, 0:NG * 128]
        onT = work[0:CH, 0:2 * SP].rearrange("p (c s) -> p c s", c=2)
        proj = work[0:TT, 0:2 * D].rearrange("p (t d) -> p t d", t=2)

        const = m.sem(X + "const")
        ready = m.sem(X + "ready")
        qk_in_place = m.transfers(X + "qk_in_place", 2 * PARTS)
        tv_in_place = m.transfers(X + "tv_in_place")
        scored_q = m.event(X + "scored_q", 12)
        maxed = m.event(X + "maxed", 12)
        max_turned = m.event(X + "max_turned")
        max_high = m.event(X + "max_high")
        max_rest = m.event(X + "max_rest")
        max_mid = m.event(X + "max_mid")
        max_low = m.event(X + "max_low")
        max_in_place = m.transfers(X + "max_in_place", 3)
        v_spread = m.event(X + "v_spread")
        scored_k = m.event(X + "scored_k", 6)
        exped = m.event(X + "exped", 6)
        summed = m.event(X + "summed", 3)
        o_copied = m.event(X + "o_copied", 3)
        o_turned = m.event(X + "o_turned", 2)
        recip = m.event(X + "recip", 2)
        o_normed = m.event(X + "o_normed", 2)
        added = m.event(X + "added")
        h_turned = m.event(X + "h_turned")
        h_copied = m.event(X + "h_copied")
        done = m.event(X + "done", 1 if causal else 3)
        high = m.event(X + "high", 2)
        left = m.event(X + "left", 2)
        middle = m.event(X + "middle", 2)
        low = m.event(X + "low", 2)
        finished = m.event(X + "finished")
        stored = m.transfers(X + "stored", 1 if causal else 2)
        block = ctx.enter_context(nc.Block())

        turn = 3 if causal else 4
        n_const, n_ready = (5 * 16, 7) if causal else (2 * 16, 3)

        def heads_of(fill):
            return fill // 6, 2 * (fill % 6)

        @block.sync
        def _(sp):
            for e in (qk_in_place, tv_in_place, max_in_place, stored):
                e.seed(sp)
            loads = [(ident[:], A["ident"])]
            if causal:
                loads += [(wout[:], A["wout"].rearrange("(c p) d -> p c d", p=CH)), (bout[:, 0], A["bout"]),
                          (masks[:, 0], A["above"]), (masks[:, 1], A["aboveT"])]
            else:
                loads += [(wqkv[:], A["wqkv2"].rearrange("(c p) d -> p c d", p=CH))]
            for to, of in loads:
                sp.dma_start(to, of).then_inc(const, 16)

            def step(c):
                b = c - 3
                if b.inside(n):
                    sp.wait_ge(max_low.sem, max_low.at(b))
                    for a in range(PARTS):
                        sp.dma_start(qs[STACK + a:STACK + a + 1, b.place], mxp[:, b.parity, a]).then_inc(max_in_place.of(b), 16)
                b = c - 6
                if b.inside(n):
                    sp.wait_ge(finished.sem, finished.at(b))
                    if causal:
                        sp.dma_start(scr["h_pre"][b.number], res[:, b.parity, 0]).then_inc(stored.of(b), 16)
                    else:
                        sp.wait_ge(added.sem, added.at(b))
                        sp.dma_start(scr["tv2"][b.number], res[:, b.parity]).then_inc(stored.of(b), 16)
                        sp.wait_ge(low.sem, low.at(b))
                        sp.dma_start(scr["qk2"][b.number].rearrange("i c a p s -> p (i c a) s"),
                                     parts[:, b.parity].rearrange("p i c a s -> p (i c a) s")).then_inc(stored.of(b), 16)
                if c.inside(n):
                    sp.wait_ge(scored_k.sem, scored_k.at(c - 4))
                    at = 0
                    for a in range(PARTS):
                        rows = slice(at, at + (PARTS - a) * DH)
                        at = rows.stop
                        for i, (stack, of) in enumerate(((qs, slice(0, PARTS - a)), (ks, slice(a, PARTS)))):
                            sp.dma_start(stack[rows, c.place].rearrange("r (c h) s -> r c (h s)", c=2),
                                         qk_in[c.number, i, :, of].rearrange("c a (d h) s -> (a d) c (h s)",
                                                                             d=DH)).then_inc(qk_in_place.of(c), 16)
                b = c - 1
                if b.inside(n):
                    sp.wait_ge(added.sem, added.at(b - 4))
                    sp.wait_ge(v_spread.sem, v_spread.at(b - 4))
                    sp.dma_start(tv[:, b.place], tv_in[b.number]).then_inc(tv_in_place.of(b), 16)
            pipeline(sp, n, 6, R, step)
            for i in range(n - R, n):
                sp.wait_ge(stored.of(Image(i // R, i % R, R)), stored.at(Image(i // R, i % R, R)))

        @block.gpsimd
        def _(pool):
            for e in (max_mid, max_low, v_spread, added, middle, low):
                e.seed(pool)
            pool.wait_ge(ready, n_ready)

            def step(c):
                b = c - 3
                if b.inside(n):
                    pool.wait_ge(max_rest.sem, max_rest.at(b))
                    pool.wait_ge(max_in_place.of(b - 2), max_in_place.at(b - 2))
                    pool.wait_ge(added.sem, added.at(c - 6))
                    m.hold(pool)
                    pool.tensor_copy(mxp[:, b.parity, 1], mxr[:, b.parity]).then_inc(max_mid.sem, 1)
                    pool.wait_ge(max_mid.sem, max_mid.at(b))
                    pool.tensor_tensor(mxp[:, b.parity, 2], mxr[:, b.parity], mxp[:, b.parity, 1],
                                       ALU.subtract).then_inc(max_low.sem, 1)
                    pool.wait_ge(tv_in_place.of(b), tv_in_place.at(b))
                    pool.wait_ge(summed.sem, summed.at(b - 4))
                    pool.wait_ge(max_low.sem, max_low.at(b))
                    m.hold(pool)
                    pool.tensor_copy(vx[:, b.place, :, :, 0:DH],
                                     tv[:, b.place, 1].rearrange("p t (h d) -> p t h d", d=DH)).then_inc(v_spread.sem, 1)
                b = c - 6
                if b.inside(n) and not causal:
                    for i in range(2):
                        pool.wait_ge(left.sem, left.at(b, i + 1))
                        if i:
                            pool.wait_ge(low.sem, low.at(b, i))
                        elif (c - 3).inside(n):
                            pool.wait_ge(v_spread.sem, v_spread.at(c - 3))
                        else:
                            pool.wait_ge(added.sem, added.at(b))
                        m.hold(pool)
                        pool.tensor_copy(parts[:, b.parity, i, :, place_of(i, 1)], rest[:, i]).then_inc(middle.sem, 1)
                        pool.wait_ge(middle.sem, middle.at(b, i + 1))
                        pool.tensor_tensor(parts[:, b.parity, i, :, place_of(i, 2)], rest[:, i],
                                           parts[:, b.parity, i, :, place_of(i, 1)], ALU.subtract).then_inc(low.sem, 1)
                b = c - 5
                if b.inside(n):
                    if not causal and (c - 6).inside(n):
                        pool.wait_ge(low.sem, low.at(c - 6))
                    elif (c - 3).inside(n):
                        pool.wait_ge(v_spread.sem, v_spread.at(c - 3))
                    pool.wait_ge(stored.of(b - 2), stored.at(b - 2))
                    if causal:
                        pool.wait_ge(tv_in_place.of(b), tv_in_place.at(b))
                        pool.tensor_tensor(res[:, b.parity, 1], tv[:, b.place, 0], bout2[:],
                                           ALU.add).then_inc(added.sem, 1)
                    else:
                        pool.wait_ge(o_normed.sem, o_normed.at(b))
                        pool.tensor_tensor(res[:, b.parity, 0], tv[:, b.place, 0], on[:, b.parity],
                                           ALU.add).then_inc(added.sem, 1)
            pipeline(pool, n, 6, R, step)

        @block.scalar
        def _(act):
            for e in (exped, o_copied, h_copied, high):
                e.seed(act)
            if not causal:
                finished.seed(act)

            def step(c):
                b4, b5, b6 = c - 4, c - 5, c - 6
                for k in range(6):
                    if b4.inside(n):
                        g, kt = k // 2, k % 2
                        rows = TT - kt
                        act.wait_ge(scored_k.sem, scored_k.at(b4, k + 1))
                        act.wait_ge(summed.sem, summed.at(b4 - 1, g + 1))
                        if causal and kt:
                            of, to = sk[k % 2][0:rows, 0, 0:G * TT], ex[0:rows, g, kt, 0:G * TT]
                        else:
                            of = sk[k % 2][0:rows, :, 0:2 * SP]
                            to = ex[0:rows, g, kt].rearrange("p (a s) -> p a s", a=2)
                        nc.scalar.activation(to, of, ACT.Exp).then_inc(exped.sem, 1)
                    if b6.inside(n):
                        if k == 1:
                            act.wait_ge(h_turned.sem, h_turned.at(b6))
                            nc.scalar.copy(hT[:], onT).then_inc(h_copied.sem, 1)
                        if k in (2, 3) and not causal:
                            i = k - 2
                            act.wait_ge(stored.of(b6 - 2), stored.at(b6 - 2))
                            act.wait_ge(done.sem, done.at(b6, i + 1))
                            split_high(nc.scalar, parts[:, b6.parity, i, :, place_of(i, 0)], onT, SCALES[i]).then_inc(high.sem, 1)
                        if k == 3 and not causal:
                            act.wait_ge(done.sem, done.at(b6, 3))
                            nc.scalar.copy(res[:, b6.parity, 1], vp).then_inc(finished.sem, 1)
                    if b5.inside(n) and k == 0:
                        act.wait_ge(summed.sem, summed.at(b5, 3))
                        nc.scalar.copy(ot[:, b5.parity, 2], pv).then_inc(o_copied.sem, 1)
                    if b4.inside(n) and k in (2, 4):
                        g = k // 2 - 1
                        act.wait_ge(summed.sem, summed.at(b4, g + 1))
                        nc.scalar.copy(ot[:, b4.parity, g], pv).then_inc(o_copied.sem, 1)
            pipeline(act, n, 6, R, step)

        @block.vector
        def _(dve):
            for e in (maxed, max_high, max_rest, recip, o_normed, left):
                e.seed(dve)
            if causal:
                finished.seed(dve)
            dve.wait_ge(const, n_const)
            nc.vector.memset(ks[STACK:AUG], 1.0).then_inc(ready, 1)
            nc.vector.memset(vx[:], 0.0).then_inc(ready, 1)
            dve.wait_ge(ready, 2)
            nc.vector.memset(vx[:, :, :, :, DH:DH + 1], 1.0).then_inc(ready, 1)
            dve.wait_ge(ready, 3)
            if causal:
                nc.vector.tensor_copy(maskb[:], masks[:]).then_inc(ready, 1)
                nc.vector.tensor_copy(identb[:], ident[0:TT, 0:TT]).then_inc(ready, 1)
                nc.vector.tensor_copy(bout2[:, 0], bout[:, 0]).then_inc(ready, 1)
                nc.vector.tensor_copy(bout2[:, 1], bout[:, 0]).then_inc(ready, 1)

            def step(c):
                b2, b3, b4, b5, b6 = (c - s for s in (2, 3, 4, 5, 6))
                for k in range(6):
                    if b2.inside(n):
                        for f in (2 * k, 2 * k + 1):
                            qt, h = heads_of(f)
                            width = (TT if qt == 0 else SP) if causal else SEQ
                            dve.wait_ge(scored_q.sem, scored_q.at(b2, f + 1))
                            nc.vector.reduce_max(mx[:, b2.parity, qt, h:h + 2], sq[f % 2][:, :, 0:width],
                                                 AX.X).then_inc(maxed.sem, 1)
                    if b3.inside(n) and k == 0:
                        dve.wait_ge(max_turned.sem, max_turned.at(b3))
                        dve.wait_ge(max_in_place.of(b3 - 2), max_in_place.at(b3 - 2))
                        nc.vector.tensor_scalar(mxp[:, b3.parity, 0], mxT, -1.0, None, ALU.mult).then_inc(max_high.sem, 1)
                        dve.wait_ge(max_high.sem, max_high.at(b3))
                        nc.vector.scalar_tensor_tensor(out=mxr[:, b3.parity], in0=mxT, scalar=-1.0,
                                                       in1=mxp[:, b3.parity, 0], op0=ALU.mult,
                                                       op1=ALU.subtract).then_inc(max_rest.sem, 1)
                    if b6.inside(n):
                        if k in (2, 3) and not causal:
                            i = k - 2
                            dve.wait_ge(high.sem, high.at(b6, i + 1))
                            dve.wait_ge(low.sem, low.at(b6 - 1, i + 1))
                            nc.vector.scalar_tensor_tensor(out=rest[:, i], in0=onT, scalar=SCALES[i],
                                                           in1=parts[:, b6.parity, i, :, place_of(i, 0)], op0=ALU.mult,
                                                           op1=ALU.subtract).then_inc(left.sem, 1)
                        if k == 2 and causal:
                            dve.wait_ge(done.sem, done.at(b6))
                            dve.wait_ge(added.sem, added.at(b6))
                            nc.vector.tensor_tensor(res[:, b6.parity, 0], proj, res[:, b6.parity, 1],
                                                    ALU.add).then_inc(finished.sem, 1)
                    if b5.inside(n) and k in (turn, turn + 1):
                        t = k - turn
                        dve.wait_ge(o_turned.sem, o_turned.at(b5, t + 1))
                        o4 = oT.rearrange("p (h e) -> p h e", e=32)
                        nc.vector.reciprocal(rec[:, t], o4[:, :, DH]).then_inc(recip.sem, 1)
                        dve.wait_ge(recip.sem, recip.at(b5, t + 1))
                        nc.vector.tensor_tensor(on[:, b5.parity, t].rearrange("p (h d) -> p h d", d=DH),
                                                o4[:, :, 0:DH], rec[:, t].unsqueeze(2).broadcast_to([TT, HEADS, DH]),
                                                ALU.mult).then_inc(o_normed.sem, 1)
            pipeline(dve, n, 6, R, step)

        @block.tensor
        def _(pe):
            for e in (scored_q, max_turned, scored_k, summed, o_turned, h_turned, done):
                e.seed(pe)
            pe.wait_ge(const, n_const)
            pe.wait_ge(ready, n_ready)

            def query_scores(b, f):
                qt, h = heads_of(f)
                bank = sq[f % 2]
                if f < 2:
                    pe.wait_ge(maxed.sem, maxed.at(b - 1, 11 + f))
                else:
                    pe.wait_ge(maxed.sem, maxed.at(b, f - 1))
                keys = TT * (qt + 1) if causal else SP
                if causal:
                    nc.tensor.matmul(bank[:, :, qt * TT:(qt + 1) * TT], identb[:], mask_of(0, 2), start=True, stop=False,
                                     skip_group_check=True)
                for j in range(2):
                    mm = nc.tensor.matmul(bank[:, j, 0:keys], qs[0:STACK, b.place, h + j, qt * TT:(qt + 1) * TT],
                                          ks[0:STACK, b.place, h + j, 0:keys], start=not causal, stop=True,
                                          skip_group_check=causal)
                mm.then_inc(scored_q.sem, 1)

            def mask_of(i, copies):
                return maskb[:, i:i + 1].broadcast_to([TT, copies, TT])

            def key_scores(b, k):
                g, kt = k // 2, k % 2
                rows = TT - kt
                buf = sk[k % 2]
                if k < 2:
                    pe.wait_ge(exped.sem, exped.at(b - 1, 5 + k))
                else:
                    pe.wait_ge(exped.sem, exped.at(b, k - 1))
                if causal and kt:
                    nc.tensor.matmul(buf[0:rows, 0, 0:G * TT].rearrange("p (h s) -> p h s", h=G),
                                     identb[:, 0:rows], mask_of(1, G), start=True, stop=False, skip_group_check=True)
                    for j in range(G):
                        mm = nc.tensor.matmul(buf[0:rows, 0, j * TT:(j + 1) * TT], ks[:, b.place, G * g + j, TT:TT + rows],
                                              qs[:, b.place, G * g + j, TT:SP], start=False, stop=True, skip_group_check=True)
                else:
                    for a in range(2):
                        if causal:
                            nc.tensor.matmul(buf[0:rows, a, 0:2 * SP].rearrange("p (h s) -> p h s", h=2)[:, :, 0:TT],
                                             identb[:, 0:rows], mask_of(1, 2), start=True, stop=False, skip_group_check=True)
                        for j in range(2):
                            h = G * g + 2 * a + j
                            mm = nc.tensor.matmul(buf[0:rows, a, j * SP:(j + 1) * SP],
                                                  ks[:, b.place, h, kt * TT:kt * TT + rows], qs[:, b.place, h, :],
                                                  start=not causal, stop=True, skip_group_check=causal)
                mm.then_inc(scored_k.sem, 1)

            def value_products(b, g):
                for kt in range(2):
                    pe.wait_ge(exped.sem, exped.at(b, 2 * g + kt + 1))
                    rows = TT - kt
                    for j in range(G):
                        if causal and kt:
                            of, to = ex[0:rows, g, kt, j * TT:(j + 1) * TT], pv[32 * j:32 * j + 32, TT:SP]
                        else:
                            of, to = ex[0:rows, g, kt, j * SP:(j + 1) * SP], pv[32 * j:32 * j + 32, 0:SP]
                        mm = nc.tensor.matmul(to, vx[0:rows, b.place, kt, G * g + j, :], of, start=(kt == 0), stop=(kt == 1),
                                              skip_group_check=causal)
                mm.then_inc(summed.sem, 1)

            def step(c):
                b2, b3, b4, b5, b6 = (c - s for s in (2, 3, 4, 5, 6))
                if b2.inside(n):
                    pe.wait_ge(qk_in_place.of(b2), qk_in_place.at(b2))
                for k in range(6):
                    if k == 0 and b4.inside(n):
                        pe.wait_ge(max_in_place.of(b4), max_in_place.at(b4))
                        pe.wait_ge(v_spread.sem, v_spread.at(b4))
                    if b4.inside(n):
                        key_scores(b4, k)
                    if b2.inside(n):
                        query_scores(b2, 2 * k)
                        query_scores(b2, 2 * k + 1)
                    if k == 0 and b3.inside(n):
                        pe.wait_ge(maxed.sem, maxed.at(b3))
                        pe.wait_ge(o_normed.sem, o_normed.at(c - 6))
                        for t in range(2):
                            mm = nc.tensor.transpose(mxT[:, t * TT:(t + 1) * TT], mx[:, b3.parity, t], ident[0:TT, 0:TT])
                        mm.then_inc(max_turned.sem, 1)
                    if k == 0 and b5.inside(n):
                        pe.wait_ge(o_copied.sem, o_copied.at(b5, 2))
                        value_products(b5, 2)
                    if b6.inside(n):
                        if k == 1:
                            if b3.inside(n):
                                pe.wait_ge(max_rest.sem, max_rest.at(b3))
                            else:
                                pe.wait_ge(o_normed.sem, o_normed.at(b6))
                            if not causal:
                                pe.wait_ge(added.sem, added.at(b6))
                            of = on[:, b6.parity] if causal else res[:, b6.parity, 0]
                            for t in range(2):
                                for h in range(2):
                                    mm = nc.tensor.transpose(onT[:, h, t * TT:(t + 1) * TT],
                                                             of[:, t, h * CH:(h + 1) * CH], ident[0:TT, 0:TT])
                            mm.then_inc(h_turned.sem, 1)
                        if k == 2:
                            pe.wait_ge(h_copied.sem, h_copied.at(b6))
                        if k == 2 and causal:
                            for t in range(2):
                                for h in range(2):
                                    mm = nc.tensor.matmul(proj[:, t], hT[:, h, t * TT:(t + 1) * TT], wout[:, h],
                                                          start=(h == 0), stop=(h == 1))
                            mm.then_inc(done.sem, 1)
                        if k in (2, 3) and not causal:
                            i = k - 2
                            if i:
                                pe.wait_ge(left.sem, left.at(b6, i))
                            for o in range(2):
                                for h in range(2):
                                    mm = nc.tensor.matmul(onT[:, o], wqkv[:, h, i * D + o * CH:i * D + (o + 1) * CH],
                                                          hT[:, h], start=(h == 0), stop=(h == 1))
                            mm.then_inc(done.sem, 1)
                        if k == 3 and not causal:
                            if b4.inside(n):
                                pe.wait_ge(o_copied.sem, o_copied.at(b4, 1))
                            elif b5.inside(n):
                                pe.wait_ge(o_copied.sem, o_copied.at(b5))
                            for t in range(2):
                                for h in range(2):
                                    mm = nc.tensor.matmul(vp[:, t], hT[:, h, t * TT:(t + 1) * TT], wqkv[:, h, 2 * D:3 * D],
                                                          start=(h == 0), stop=(h == 1))
                            mm.then_inc(done.sem, 1)
                    if b4.inside(n) and k in (2, 4):
                        g = k // 2 - 1
                        if g:
                            pe.wait_ge(o_copied.sem, o_copied.at(b4, g))
                            if not causal and b6.inside(n):
                                pe.wait_ge(finished.sem, finished.at(b6))
                        else:
                            pe.wait_ge(o_copied.sem, o_copied.at(b4 - 1))
                        value_products(b4, g)
                    if b5.inside(n) and k in (turn, turn + 1):
                        t = k - turn
                        if t:
                            pe.wait_ge(o_normed.sem, o_normed.at(b5, 1))
                        else:
                            pe.wait_ge(o_copied.sem, o_copied.at(b5))
                            if b6.inside(n):
                                if causal:
                                    pe.wait_ge(finished.sem, finished.at(b6))
                                else:
                                    pe.wait_ge(left.sem, left.at(b6))
                            elif b3.inside(n):
                                pe.wait_ge(max_rest.sem, max_rest.at(b3))
                        for g in range(NG):
                            mm = nc.tensor.transpose(oT[:, g * 128:(g + 1) * 128], ot[:, b5.parity, g, t * TT:(t + 1) * TT],
                                                     ident[:, :])
                        mm.then_inc(o_turned.sem, 1)
            pipeline(pe, n, 6, R, step)


def route_pass(nc, n, A, scr, y_all):
    R = 8
    DEPTH = 10
    with ExitStack() as ctx:
        m = Memory(nc, ctx, R)
        ident = m.sb("r_ident", [128, 128])
        normw = m.sb("r_normw", [TT, D])
        slots = m.sb("r_slots", [SLOTS, D])
        slots2 = m.sb("r_slots2", [SLOTS, D])
        scale = m.sb("r_scale", [SLOTS, 4])
        slotsT = m.sb("r_slotsT", [CH, 2, SLOTS])
        half = m.sb("r_half", [TT, 2])
        hp = m.sb("r_hp", [TT, R, 2, D])
        h2 = m.sb("r_h2", [TT, R, 2, D])
        xn = m.sb("r_xn", [TT, R, 2, D])
        junk = m.sb("r_junk", [TT, 2, 2, D])
        junk2 = m.sb("r_junk2", [TT, 2, 2, D])
        bn = m.sb("r_bn", [TT, 2, 6])
        mv = m.sb("r_mv", [TT, R, 2, 2])
        st = m.sb("r_st", [TT, R, 12, 2])
        ex = m.sb("r_ex", [SLOTS, R, 4])
        xnT = m.sb("r_xnT", [CH, 2, 2, SP])
        lg = m.sb("r_lg", [TT, R, 2, SLOTS])
        cw = m.sb("r_cw", [TT, R, 2, SLOTS])
        dw = m.sb("r_dw", [SLOTS, R, SP])
        cT = m.sb("r_cT", [SLOTS, R, SP])
        dT = m.sb("r_dT", [TT, 2, 2, SLOTS])
        VAR, RSTD, SS, RIN, RMS, NN, NIN, RN, NMAX, DEN, RDEN = range(11)
        xtp = m.ps("r_xtp", [CH, 2, SP])
        lgp = m.ps("r_lgp", [TT, 2, SLOTS])
        lgT = m.ps("r_lgT", [SLOTS, SP])
        cTp = m.ps("r_cTp", [SLOTS, SP])
        dTp = m.ps("r_dTp", [TT, 2, SLOTS])
        yp = m.ps("r_yp", [CH, 2, SLOTS])

        const = m.sem("r_const")
        prep = m.sem("r_prep")
        prep_pow = m.sem("r_prep_pow")
        prep_turned = m.sem("r_prep_turned")
        loaded = m.transfers("r_loaded")
        stats = m.event("r_stats", 2)
        mean_var = m.event("r_mean_var", 2)
        var_eps = m.event("r_var_eps")
        rstd = m.event("r_rstd")
        normed = m.event("r_normed", 2)
        squared = m.event("r_squared", 2)
        ms_eps = m.event("r_ms_eps")
        rms = m.event("r_rms")
        scaled = m.event("r_scaled", 2)
        squared2 = m.event("r_squared2", 2)
        guarded = m.event("r_guarded")
        rnorm = m.event("r_rnorm")
        x_turned = m.event("r_x_turned")
        x_copied = m.event("r_x_copied")
        product = m.event("r_product")
        logits = m.event("r_logits")
        logits_turned = m.event("r_logits_turned")
        maxed = m.event("r_maxed", 2)
        exped = m.event("r_exped", 3)
        recip = m.event("r_recip", 2)
        combine = m.event("r_combine")
        dispatch = m.event("r_dispatch")
        w_turned = m.event("r_w_turned", 2)
        w_copied = m.event("r_w_copied", 2)
        y_done = m.event("r_y_done")
        y_copied = m.event("r_y_copied")
        stored = m.transfers("r_stored", 2)
        block = ctx.enter_context(nc.Block())

        @block.sync
        def _(sp):
            for e in (loaded, stored):
                e.seed(sp)
            for to, of in ((ident[:], A["ident"]), (normw[:], A["normw"]), (slots[:], A["slots"]),
                           (scale[:, 0:1], A["scale"])):
                sp.dma_start(to, of).then_inc(const, 16)

            def step(c):
                if c.inside(n):
                    sp.wait_ge(normed.sem, normed.at(c - R))
                    sp.dma_start(hp[:, c.place], scr["h_pre"][c.number]).then_inc(loaded.of(c), 16)
                b = c - 9
                if b.inside(n):
                    sp.wait_ge(normed.sem, normed.at(b))
                    sp.dma_start(scr["h2"][b.number], h2[:, b.place]).then_inc(stored.of(b), 16)
                    sp.wait_ge(w_copied.sem, w_copied.at(b, 1))
                    sp.dma_start(scr["mix"][b.number, :, D:D + SP], cT[:, b.place]).then_inc(stored.of(b), 16)
            pipeline(sp, n, DEPTH, R, step)
            for i in range(n - R, n):
                sp.wait_ge(stored.of(Image(i // R, i % R, R)), stored.at(Image(i // R, i % R, R)))

        @block.gpsimd
        def _(pool):
            for e in (rstd, rms, rnorm, combine):
                e.seed(pool)
            pool.wait_ge(prep, 4)
            pool.tensor_tensor(scale[:, 2:3], scale[:, 1:2], half[0:SLOTS, 0:1], ALU.pow).then_inc(prep_pow, 1)
            pool.wait_ge(prep_pow, 1)

            def step(c):
                b1, b3, b5, b8 = c - 1, c - 3, c - 5, c - 8
                if b8.inside(n):
                    pool.wait_ge(recip.sem, recip.at(b8, 1))
                    pool.tensor_tensor(cw[:, b8.place], cw[:, b8.place],
                                       st[:, b8.place, RDEN].unsqueeze(2).broadcast_to([TT, 2, SLOTS]),
                                       ALU.mult).then_inc(combine.sem, 1)
                if b1.inside(n):
                    pool.wait_ge(var_eps.sem, var_eps.at(b1))
                    pool.tensor_tensor(st[:, b1.place, RSTD], st[:, b1.place, VAR], half[:], ALU.pow).then_inc(rstd.sem, 1)
                if b3.inside(n):
                    pool.wait_ge(ms_eps.sem, ms_eps.at(b3))
                    pool.tensor_tensor(st[:, b3.place, RMS], st[:, b3.place, RIN], half[:], ALU.pow).then_inc(rms.sem, 1)
                if b5.inside(n):
                    pool.wait_ge(guarded.sem, guarded.at(b5))
                    pool.tensor_tensor(st[:, b5.place, RN], st[:, b5.place, NIN], half[:], ALU.pow).then_inc(rnorm.sem, 1)
            pipeline(pool, n, DEPTH, R, step)

        @block.scalar
        def _(act):
            for e in (squared, squared2, x_copied, exped, w_copied):
                e.seed(act)
            act.wait_ge(prep, 3)

            def step(c):
                b2, b4, b5, b7, b9 = c - 2, c - 4, c - 5, c - 7, c - 9
                if b7.inside(n):
                    act.wait_ge(maxed.sem, maxed.at(b7, 1))
                    for t in range(2):
                        nc.scalar.activation(cw[:, b7.place, t], lg[:, b7.place, t], ACT.Exp, bias=st[:, b7.place, NMAX, t:t + 1],
                                             accum_out=st[:, b7.place, DEN, t:t + 1]).then_inc(exped.sem, 1)
                if b5.inside(n):
                    act.wait_ge(x_turned.sem, x_turned.at(b5))
                    nc.scalar.copy(xnT[:, b5.parity], xtp[:]).then_inc(x_copied.sem, 1)
                if b2.inside(n):
                    for t in range(2):
                        act.wait_ge(normed.sem, normed.at(b2, t + 1))
                        nc.scalar.activation(junk[:, b2.parity, t], h2[:, b2.place, t], ACT.Square,
                                             accum_out=st[:, b2.place, SS, t:t + 1]).then_inc(squared.sem, 1)
                if b7.inside(n):
                    act.wait_ge(maxed.sem, maxed.at(b7, 2))
                    nc.scalar.activation(dw[:, b7.place, 0:SEQ], lgT[:, 0:SEQ], ACT.Exp, bias=ex[:, b7.place, 0:1],
                                         accum_out=ex[:, b7.place, 1:2]).then_inc(exped.sem, 1)
                if b9.inside(n):
                    act.wait_ge(stored.of(b9 - R), stored.at(b9 - R))
                    act.wait_ge(w_turned.sem, w_turned.at(b9, 1))
                    nc.scalar.copy(cT[:, b9.place], cTp[:]).then_inc(w_copied.sem, 1)
                    act.wait_ge(w_turned.sem, w_turned.at(b9, 2))
                    nc.scalar.copy(dT[:, b9.parity], dTp[:]).then_inc(w_copied.sem, 1)
                if b4.inside(n):
                    for t in range(2):
                        act.wait_ge(scaled.sem, scaled.at(b4, t + 1))
                        nc.scalar.activation(junk2[:, b4.parity, t], xn[:, b4.place, t], ACT.Square,
                                             accum_out=st[:, b4.place, NN, t:t + 1]).then_inc(squared2.sem, 1)
            pipeline(act, n, DEPTH, R, step)

        @block.vector
        def _(dve):
            for e in (stats, mean_var, var_eps, normed, ms_eps, scaled, guarded, logits, maxed, recip, dispatch, y_copied):
                e.seed(dve)
            dve.wait_ge(const, 64)
            nc.vector.memset(half[:], -0.5).then_inc(prep, 1)
            nc.vector.memset(dw[:], 0.0).then_inc(prep, 1)
            nc.vector.tensor_tensor_reduce(out=slots2[:], in0=slots[:], in1=slots[:], scale=1.0, scalar=0.0,
                                           op0=ALU.mult, op1=ALU.add, accum_out=scale[:, 3:4]).then_inc(prep, 1)
            dve.wait_ge(prep, 3)
            nc.vector.tensor_scalar(scale[:, 1:2], scale[:, 3:4], 1e-10, None, ALU.max).then_inc(prep, 1)
            dve.wait_ge(prep_pow, 1)
            nc.vector.tensor_scalar(slots2[:], slots[:], scale[:, 2:3], scale[:, 0:1], ALU.mult, ALU.mult).then_inc(prep, 1)
            dve.wait_ge(prep_turned, 1)
            nc.vector.tensor_copy(slotsT[:], xtp[:, :, 0:SLOTS]).then_inc(prep, 1)

            def step(c):
                b1, b2, b3, b4, b5, b6, b7, b8, b10 = (c - s for s in (1, 2, 3, 4, 5, 6, 7, 8, 10))
                if b2.inside(n):
                    p = b2.place
                    dve.wait_ge(rstd.sem, rstd.at(b2))
                    dve.wait_ge(stored.of(b2 - R), stored.at(b2 - R))
                    for t in range(2):
                        nc.vector.tensor_scalar(h2[:, p, t], hp[:, p, t], mv[:, p, t, 0:1], st[:, p, RSTD, t:t + 1],
                                                ALU.subtract, ALU.mult).then_inc(normed.sem, 1)
                if b7.inside(n):
                    dve.wait_ge(logits_turned.sem, logits_turned.at(b7))
                    nc.vector.tensor_reduce(ex[:, b7.place, 0:1], lgT[:, 0:SEQ], AX.X, ALU.max, negate=True).then_inc(maxed.sem, 1)
                if b4.inside(n):
                    p = b4.place
                    dve.wait_ge(rms.sem, rms.at(b4))
                    for t in range(2):
                        nc.vector.scalar_tensor_tensor(out=xn[:, p, t], in0=h2[:, p, t], scalar=st[:, p, RMS, t:t + 1],
                                                       in1=normw[:], op0=ALU.mult, op1=ALU.mult).then_inc(scaled.sem, 1)
                if b8.inside(n):
                    p = b8.place
                    dve.wait_ge(exped.sem, exped.at(b8, 3))
                    nc.vector.reciprocal(st[:, p, RDEN], st[:, p, DEN]).then_inc(recip.sem, 1)
                    nc.vector.reciprocal(ex[:, p, 2:3], ex[:, p, 1:2]).then_inc(recip.sem, 1)
                if b1.inside(n):
                    dve.wait_ge(loaded.of(b1), loaded.at(b1))
                    for t in range(2):
                        nc.vector.bn_stats(out=bn[:, t], in_=hp[:, b1.place, t]).then_inc(stats.sem, 1)
                if b8.inside(n):
                    p = b8.place
                    dve.wait_ge(recip.sem, recip.at(b8))
                    nc.vector.tensor_scalar(dw[:, p, 0:SEQ], dw[:, p, 0:SEQ], ex[:, p, 2:3], None, ALU.mult).then_inc(dispatch.sem, 1)
                if b1.inside(n):
                    for t in range(2):
                        dve.wait_ge(stats.sem, stats.at(b1, t + 1))
                        m.hold(dve)
                        nc.vector.bn_aggr(out=mv[:, b1.place, t], in_=bn[:, t]).then_inc(mean_var.sem, 1)
                if b3.inside(n):
                    dve.wait_ge(squared.sem, squared.at(b3))
                    nc.vector.tensor_scalar(st[:, b3.place, RIN], st[:, b3.place, SS], 1.0 / D, LN_EPS,
                                            ALU.mult, ALU.add).then_inc(ms_eps.sem, 1)
                if b5.inside(n):
                    dve.wait_ge(squared2.sem, squared2.at(b5))
                    nc.vector.tensor_scalar(st[:, b5.place, NIN], st[:, b5.place, NN], 1e-10, None, ALU.max).then_inc(guarded.sem, 1)
                if b1.inside(n):
                    dve.wait_ge(mean_var.sem, mean_var.at(b1))
                    nc.vector.tensor_scalar(st[:, b1.place, VAR], mv[:, b1.place, :, 1], LN_EPS, None, ALU.add).then_inc(var_eps.sem, 1)
                if b6.inside(n):
                    p = b6.place
                    dve.wait_ge(product.sem, product.at(b6))
                    dve.wait_ge(rnorm.sem, rnorm.at(b6))
                    nc.vector.tensor_tensor(lg[:, p], lgp[:], st[:, p, RN].unsqueeze(2).broadcast_to([TT, 2, SLOTS]),
                                            ALU.mult).then_inc(logits.sem, 1)
                if b10.inside(n):
                    dve.wait_ge(y_done.sem, y_done.at(b10))
                    nc.vector.tensor_copy(y_all[:, :, :, b10.number], yp[:]).then_inc(y_copied.sem, 1)
                if b6.inside(n):
                    dve.wait_ge(logits.sem, logits.at(b6))
                    nc.vector.tensor_reduce(st[:, b6.place, NMAX], lg[:, b6.place], AX.X, ALU.max, negate=True).then_inc(maxed.sem, 1)
            pipeline(dve, n, DEPTH, R, step)

        @block.tensor
        def _(pe):
            for e in (x_turned, product, logits_turned, w_turned, y_done):
                e.seed(pe)
            pe.wait_ge(prep, 5)
            pe.wait_ge(const, 64)
            for h in range(2):
                mm = nc.tensor.transpose(xtp[:, h, 0:SLOTS], slots2[:, h * CH:(h + 1) * CH], ident[0:SLOTS, 0:SLOTS])
            mm.then_inc(prep_turned, 1)
            pe.wait_ge(prep, 6)

            def step(c):
                b5, b6, b7, b9, b10 = c - 5, c - 6, c - 7, c - 9, c - 10
                if b7.inside(n):
                    pe.wait_ge(logits.sem, logits.at(b7))
                    pe.wait_ge(exped.sem, exped.at(b7 - 1))
                    m.hold(pe)
                    for t in range(2):
                        mm = nc.tensor.transpose(lgT[:, t * TT:(t + 1) * TT], lg[:, b7.place, t], ident[0:TT, 0:TT])
                    mm.then_inc(logits_turned.sem, 1)
                if b5.inside(n):
                    pe.wait_ge(scaled.sem, scaled.at(b5))
                    pe.wait_ge(x_copied.sem, x_copied.at(b5 - 1))
                    for t in range(2):
                        for h in range(2):
                            mm = nc.tensor.transpose(xtp[:, h, t * TT:(t + 1) * TT], xn[:, b5.place, t, h * CH:(h + 1) * CH],
                                                     ident[0:TT, 0:TT])
                    mm.then_inc(x_turned.sem, 1)
                if b10.inside(n):
                    pe.wait_ge(w_copied.sem, w_copied.at(b10))
                    pe.wait_ge(y_copied.sem, y_copied.at(b10 - 1))
                    for h in range(2):
                        for t in range(2):
                            mm = nc.tensor.matmul(yp[:, h], xn[:, b10.place, t, h * CH:(h + 1) * CH], dT[:, b10.parity, t],
                                                  start=(t == 0), stop=(t == 1))
                    mm.then_inc(y_done.sem, 1)
                if b9.inside(n):
                    pe.wait_ge(combine.sem, combine.at(b9))
                    pe.wait_ge(dispatch.sem, dispatch.at(b9))
                    pe.wait_ge(w_copied.sem, w_copied.at(b9 - 1))
                    m.hold(pe)
                    for t in range(2):
                        mm = nc.tensor.transpose(cTp[:, t * TT:(t + 1) * TT], cw[:, b9.place, t], ident[0:TT, 0:TT])
                    mm.then_inc(w_turned.sem, 1)
                    for t in range(2):
                        mm = nc.tensor.transpose(dTp[:, t], dw[:, b9.place, t * TT:(t + 1) * TT], ident[0:SLOTS, 0:SLOTS])
                    mm.then_inc(w_turned.sem, 1)
                if b6.inside(n):
                    pe.wait_ge(x_copied.sem, x_copied.at(b6))
                    pe.wait_ge(logits.sem, logits.at(b6 - 1))
                    for t in range(2):
                        for h in range(2):
                            mm = nc.tensor.matmul(lgp[:, t], xnT[:, b6.parity, h, t * TT:(t + 1) * TT], slotsT[:, h],
                                                  start=(h == 0), stop=(h == 1))
                    mm.then_inc(product.sem, 1)
            pipeline(pe, n, DEPTH, R, step)


def expert_pass(nc, n, A, scr, y_all):
    R = 4
    with ExitStack() as ctx:
        m = Memory(nc, ctx, R)
        w1 = m.sb("x_w1", [CH, R, 2, FF])
        w2 = m.sb("x_w2", [128, R, FC, D])
        b1 = m.sb("x_b1", [128, SLOTS, FC])
        bias = m.sb("x_bias", [128, R, FC])
        ys = m.sb("x_ys", [CH, R, 2, n])
        hid = m.sb("x_hid", [128, 2, FC, n])
        o = m.sb("x_o", [n, R, D])
        hp = [m.ps(f"x_hp{i}", [128, 2, n]) for i in range(FC // 2)]
        op = [m.ps(f"x_op{i}", [n, D]) for i in range(2)]
        const = m.sem("x_const")
        loaded = m.transfers("x_loaded", 2)
        picked = m.event("x_picked", 2)
        hidden = m.event("x_hidden", FC // 2)
        active = m.event("x_active", FC // 2)
        done = m.event("x_done")
        copied = m.event("x_copied")
        stored = m.transfers("x_stored")
        block = ctx.enter_context(nc.Block())

        @block.sync
        def _(sp):
            for e in (loaded, stored):
                e.seed(sp)
            sp.dma_start(b1[:], A["fc1b"]).then_inc(const, 16)

            def step(c):
                if c.inside(SLOTS):
                    sp.wait_ge(done.sem, done.at(c - 4))
                    sp.dma_start(w1[:, c.place], A["fc1"][c.number].rearrange("(c p) f -> p c f", p=CH)).then_inc(loaded.of(c), 16)
                    sp.dma_start(w2[:, c.place], A["fc2"][c.number].rearrange("(k p) d -> p k d", p=128)).then_inc(loaded.of(c), 16)
                b = c - 4
                if b.inside(SLOTS):
                    sp.wait_ge(copied.sem, copied.at(b))
                    sp.dma_start(scr["mix"][:, b.number, 0:D], o[:, b.place]).then_inc(stored.of(b), 16)
            pipeline(sp, SLOTS, 4, R, step)
            for i in range(SLOTS - R, SLOTS):
                sp.wait_ge(stored.of(Image(i // R, i % R, R)), stored.at(Image(i // R, i % R, R)))

        @block.gpsimd
        def _(pool):
            picked.seed(pool)
            pool.wait_ge(const, 16)

            def step(c):
                b = c - 1
                if b.inside(SLOTS):
                    pool.wait_ge(hidden.sem, hidden.at(b - 4))
                    pool.wait_ge(active.sem, active.at(b - 4))
                    pool.wait_ge(picked.sem, picked.at(b - 1))
                    m.hold(pool)
                    pool.tensor_copy(ys[:, b.place], y_all[:, :, b.number, :]).then_inc(picked.sem, 1)
                    pool.wait_ge(picked.sem, picked.at(b, 1))
                    m.hold(pool)
                    pool.tensor_copy(bias[:, b.place], b1[:, b.number, :]).then_inc(picked.sem, 1)
            pipeline(pool, SLOTS, 4, R, step)

        @block.scalar
        def _(act):
            active.seed(act)

            def step(c):
                b = c - 2
                if b.inside(SLOTS):
                    act.wait_ge(picked.sem, picked.at(b))
                    act.wait_ge(done.sem, done.at(b - 2))
                    for i in range(FC // 2):
                        act.wait_ge(hidden.sem, hidden.at(b, i + 1))
                        for k in range(2):
                            a = nc.scalar.activation(hid[:, b.parity, 2 * i + k], hp[i][:, k], ACT.Gelu,
                                                     bias=bias[:, b.place, 2 * i + k:2 * i + k + 1])
                        a.then_inc(active.sem, 1)
            pipeline(act, SLOTS, 4, R, step)

        @block.vector
        def _(dve):
            copied.seed(dve)

            def step(c):
                b = c - 3
                if b.inside(SLOTS):
                    dve.wait_ge(done.sem, done.at(b))
                    dve.wait_ge(stored.of(b - 4), stored.at(b - 4))
                    nc.vector.tensor_copy(o[:, b.place], op[b.parity][:]).then_inc(copied.sem, 1)
            pipeline(dve, SLOTS, 4, R, step)

        @block.tensor
        def _(pe):
            for e in (hidden, done):
                e.seed(pe)

            def step(c):
                b = c - 2
                if b.inside(SLOTS):
                    pe.wait_ge(loaded.of(b), loaded.at(b))
                    pe.wait_ge(picked.sem, picked.at(b, 1))
                    for i in range(FC // 2):
                        pe.wait_ge(active.sem, active.at(b - 1, i + 1))
                        for k in range(2):
                            f = 2 * i + k
                            for h in range(2):
                                mm = nc.tensor.matmul(hp[i][:, k], w1[:, b.place, h, f * 128:(f + 1) * 128],
                                                      ys[:, b.place, h], start=(h == 0), stop=(h == 1))
                        mm.then_inc(hidden.sem, 1)
                b = c - 3
                if b.inside(SLOTS):
                    pe.wait_ge(active.sem, active.at(b))
                    pe.wait_ge(copied.sem, copied.at(b - 2))
                    for k in range(FC):
                        mm = nc.tensor.matmul(op[b.parity][:], hid[:, b.parity, k], w2[:, b.place, k],
                                              start=(k == 0), stop=(k == FC - 1))
                    mm.then_inc(done.sem, 1)
            pipeline(pe, SLOTS, 4, R, step)


def combine_pass(nc, n, A, scr, out):
    R = 4
    DEPTH = 6
    W = 2
    n = n // W
    with ExitStack() as ctx:
        m = Memory(nc, ctx, R)
        b2 = m.sb("o_b2", [SLOTS, D])
        mix = m.sb("o_mix", [SLOTS, R, W, D + SP])
        yb = m.sb("o_yb", [SLOTS, R, W, D])
        h2 = m.sb("o_h2", [TT, R, W, 2, D])
        z = m.sb("o_z", [TT, R, W, 2, D])
        res = m.sb("o_res", [TT, R, W, 2, D])
        bn = m.sb("o_bn", [TT, 2, W, 2, 6])
        mv = m.sb("o_mv", [TT, R, W, 2, 2])
        st = m.sb("o_st", [TT, R, 2, W, 2])
        half = m.sb("o_half", [TT, W, 2])
        zp = [m.ps(f"o_zp{i}", [TT, W, 512]) for i in range(4)]
        zv = [p[:, :, 0:2 * D].rearrange("p w (t d) -> p w t d", t=2) for p in zp]
        const = m.sem("o_const")
        ready = m.sem("o_ready")
        loaded = m.transfers("o_loaded", 2)
        biased = m.event("o_biased")
        mixed = m.event("o_mixed")
        summed = m.event("o_summed")
        stats = m.event("o_stats", 2 * W)
        mean_var = m.event("o_mean_var", 2 * W)
        var_eps = m.event("o_var_eps")
        rstd = m.event("o_rstd")
        normed = m.event("o_normed", 2 * W)
        stored = m.transfers("o_stored", 2)
        block = ctx.enter_context(nc.Block())

        def pair(of, unit):
            return of.rearrange("(u w) a b -> u w a b", w=W)[unit.number] if len(of.shape) == 3 else \
                of.rearrange("(u w) a b c -> u w a b c", w=W)[unit.number]

        @block.sync
        def _(sp):
            for e in (loaded, stored):
                e.seed(sp)
            sp.dma_start(b2[:], A["fc2b"]).then_inc(const, 16)

            def step(c):
                if c.inside(n):
                    sp.wait_ge(mixed.sem, mixed.at(c - R))
                    sp.wait_ge(summed.sem, summed.at(c - R))
                    sp.dma_start(mix[:, c.place], pair(scr["mix"], c).rearrange("w e x -> e w x")).then_inc(loaded.of(c), 16)
                    sp.dma_start(h2[:, c.place].rearrange("p w t d -> p w (t d)"),
                                 pair(scr["h2"], c).rearrange("w p t d -> p w (t d)")).then_inc(loaded.of(c), 16)
                b = c - DEPTH
                if b.inside(n):
                    sp.wait_ge(normed.sem, normed.at(b))
                    for t in range(2):
                        sp.dma_start(pair(out, b)[:, t * TT:min(SEQ, (t + 1) * TT)].rearrange("w p d -> p w d"),
                                     res[0:TT - t, b.place, :, t]).then_inc(stored.of(b), 16)
            pipeline(sp, n, DEPTH, R, step)
            for i in range(n - R, n):
                sp.wait_ge(stored.of(Image(i // R, i % R, R)), stored.at(Image(i // R, i % R, R)))

        @block.gpsimd
        def _(pool):
            for e in (biased, rstd):
                e.seed(pool)
            pool.wait_ge(const, 16)
            pool.wait_ge(ready, 1)

            def step(c):
                b = c - 1
                if b.inside(n):
                    pool.wait_ge(loaded.of(b), loaded.at(b))
                    pool.wait_ge(mixed.sem, mixed.at(b - R))
                    if (c - 5).inside(n):
                        pool.wait_ge(rstd.sem, rstd.at(c - 5))
                    pool.tensor_tensor(yb[:, b.place], mix[:, b.place, :, 0:D],
                                       b2[:].unsqueeze(1).broadcast_to([SLOTS, W, D]), ALU.add).then_inc(biased.sem, 1)
                b = c - 4
                if b.inside(n):
                    pool.wait_ge(var_eps.sem, var_eps.at(b))
                    if (c - 1).inside(n):
                        pool.wait_ge(biased.sem, biased.at(c - 1))
                    pool.tensor_tensor(st[:, b.place, 1], st[:, b.place, 0], half[:], ALU.pow).then_inc(rstd.sem, 1)
            pipeline(pool, n, DEPTH, R, step)

        @block.vector
        def _(dve):
            for e in (summed, stats, mean_var, var_eps, normed):
                e.seed(dve)
            nc.vector.memset(half[:], -0.5).then_inc(ready, 1)

            def step(c):
                b3, b4, b5 = c - 3, c - 4, c - 5
                tiles = [(w, t) for w in range(W) for t in range(2)]
                if b3.inside(n):
                    dve.wait_ge(mixed.sem, mixed.at(b3))
                    dve.wait_ge(loaded.of(b3), loaded.at(b3))
                    nc.vector.tensor_tensor(z[:, b3.place], zv[b3.place], h2[:, b3.place], ALU.add).then_inc(summed.sem, 1)
                if b4.inside(n):
                    for i, (w, t) in enumerate(tiles):
                        dve.wait_ge(stats.sem, stats.at(b4, i + 1))
                        m.hold(dve)
                        nc.vector.bn_aggr(out=mv[:, b4.place, w, t], in_=bn[:, b4.parity, w, t]).then_inc(mean_var.sem, 1)
                if b5.inside(n):
                    dve.wait_ge(rstd.sem, rstd.at(b5))
                    dve.wait_ge(stored.of(b5 - R), stored.at(b5 - R))
                for w in range(W):
                    if b5.inside(n):
                        for t in range(2):
                            nc.vector.tensor_scalar(res[:, b5.place, w, t], z[:, b5.place, w, t], mv[:, b5.place, w, t, 0:1],
                                                    st[:, b5.place, 1, w, t:t + 1], ALU.subtract, ALU.mult).then_inc(normed.sem, 1)
                    if b4.inside(n) and w == 0:
                        dve.wait_ge(mean_var.sem, mean_var.at(b4))
                        nc.vector.tensor_scalar(st[:, b4.place, 0], mv[:, b4.place, :, :, 1], LN_EPS, None, ALU.add).then_inc(var_eps.sem, 1)
                if b3.inside(n):
                    dve.wait_ge(summed.sem, summed.at(b3))
                    for w, t in tiles:
                        nc.vector.bn_stats(out=bn[:, b3.parity, w, t], in_=z[:, b3.place, w, t]).then_inc(stats.sem, 1)
            pipeline(dve, n, DEPTH, R, step)

        @block.tensor
        def _(pe):
            mixed.seed(pe)

            def step(c):
                b = c - 2
                if b.inside(n):
                    pe.wait_ge(biased.sem, biased.at(b))
                    pe.wait_ge(loaded.of(b), loaded.at(b))
                    pe.wait_ge(summed.sem, summed.at(b - 4))
                    for w in range(W):
                        for t in range(2):
                            mm = nc.tensor.matmul(zv[b.place][:, w, t], mix[:, b.place, w, D + t * TT:D + (t + 1) * TT],
                                                  yb[:, b.place, w], start=True, stop=True)
                    mm.then_inc(mixed.sem, 1)
            pipeline(pe, n, DEPTH, R, step)


def route_and_experts(nc, n, A, scr):
    with nc.sbuf_tensor("y_all", [CH, 2, SLOTS, n], F32) as y_all:
        route_pass(nc, n, A, scr, y_all)
        expert_pass(nc, n, A, scr, y_all)


def scratch(nc, n, kind="Internal"):
    shapes = {"tv1": ([n, TT, 2, 2, D], F32), "tv2": ([n, TT, 2, 2, D], F32),
              "qk1": ([n, 2, 2, PARTS, CH, SP], BF16), "qk2": ([n, 2, 2, PARTS, CH, SP], BF16),
              "max1": ([n, PARTS, HEADS, SP], BF16), "max2": ([n, PARTS, HEADS, SP], BF16),
              "h_pre": ([n, TT, 2, D], F32), "h2": ([n, TT, 2, D], F32),
              "mix": ([n, SLOTS, D + SP], F32)}
    return {k: nc.dram_tensor(f"scr_{k}", s, t, kind=kind).ap() for k, (s, t) in shapes.items()}


def position_table():
    i = np.arange(SEQ, dtype=np.float32)[:, None]
    j = np.arange(D, dtype=np.float32)[None, :]
    even = np.power(np.float32(10000.0), j / D).astype(np.float32)
    odd = np.power(np.float32(10000.0), (j - 1.0) / D).astype(np.float32)
    table = np.zeros((SP, D), np.float32)
    table[:SEQ] = np.where(np.arange(D)[None, :] % 2 == 0, np.sin(i / even), np.cos(i / odd))
    return table


def lay_out(x, v):
    def padded(a):
        out = np.zeros((SP, D), np.float32)
        out[:SEQ] = a
        return out

    rowb = np.zeros((SP, D), np.float32)
    rowb[0] = v["L0_tok_class_token"][0]
    rowb[1:SEQ] = v["L0_tok_b_map"][None]
    wqkv1 = np.zeros((CH + 1, 3, 2, CH), np.float32)
    for i, (w, b) in enumerate((("Wq", "bq"), ("Wk", "bk"), ("Wv", "bv"))):
        for h in range(HEADS):
            c, r = h // HC, (h % HC) * DH
            to = slice(r, r + DH) if w == "Wv" else slice(h % HC, CH, HC)
            wqkv1[r:r + DH, i, c, to] = v["L0_tok_" + w][h].T
            wqkv1[CH, i, c, to] = v["L0_tok_" + b][h]
    wqkv2 = np.array(v["L0_attn_W_qkv"])
    for i in range(4):
        cols = wqkv2[:, i * CH:(i + 1) * CH].reshape(D, HC, DH)
        wqkv2[:, i * CH:(i + 1) * CH] = cols.transpose(0, 2, 1).reshape(D, CH)
    above = np.where(np.arange(TT)[None, :] > np.arange(TT)[:, None], np.float32(MASKED), np.float32(0))
    return {
        "x": np.ascontiguousarray(x).reshape(x.shape[0], PATCHES, INPUT),
        "wmapT": np.ascontiguousarray(v["L0_tok_W_map"].T),
        "wqkv1": wqkv1,
        "pos": position_table(), "rowb": rowb,
        "lnw": padded(v["L0_tok_ln_w"]), "lnb": padded(v["L0_tok_ln_b"]),
        "ident": np.eye(128, dtype=np.float32),
        "above": above, "aboveT": np.ascontiguousarray(above.T),
        "wqkv2": wqkv2, "wout": v["L0_attn_W_out"],
        "bout": np.ascontiguousarray(np.broadcast_to(v["L0_attn_b_out"], (TT, D))),
        "slots": v["L0_ffn_slots"], "scale": np.ascontiguousarray(v["L0_ffn_scale"][:, None]),
        "normw": np.ascontiguousarray(np.broadcast_to(v["L0_ffn_norm_weight"], (TT, D))),
        "fc1": v["L0_ffn_fc1_weight"], "fc2": v["L0_ffn_fc2_weight"],
        "fc1b": np.ascontiguousarray(v["L0_ffn_fc1_bias"].reshape(SLOTS, FC, 128).transpose(2, 0, 1)),
        "fc2b": v["L0_ffn_fc2_bias"],
    }


def build(nc, A, n, out):
    scr = scratch(nc, n)
    embed_pass(nc, n, A, scr)
    attend_pass(nc, n, A, scr, causal=False)
    attend_pass(nc, n, A, scr, causal=True)
    route_and_experts(nc, n, A, scr)
    combine_pass(nc, n, A, scr, out)


def kernel(x, **weights):
    import concourse.bacc as bacc
    from concourse.bass_utils import run_bass_kernel_spmd

    arrays = lay_out(np.asarray(x), {k: np.asarray(a) for k, a in weights.items()})
    n = arrays["x"].shape[0]
    nc = bacc.Bacc("TRN2", target_bir_lowering=False, num_devices=1)
    A = {k: nc.dram_tensor(f"in_{k}", list(a.shape), mybir.dt.from_np(a.dtype), kind="ExternalInput").ap()
         for k, a in arrays.items()}
    out = nc.dram_tensor("out", [n, SEQ, D], F32, kind="ExternalOutput").ap()
    build(nc, A, n, out)
    r = run_bass_kernel_spmd(nc, [{f"in_{k}": a for k, a in arrays.items()}], core_ids=[0])
    return r.results[0]["out"]
```
